# Optimizing a Trainium2 kernel written in Bass

```python
import numpy as np
import jax
import jax.numpy as jnp

def _softmax(x, axis=-1):
    return jax.nn.softmax(x, axis=axis)

def _gelu(x):
    return jax.nn.gelu(x, approximate=True)

def _silu(x):
    return jax.nn.silu(x)

def _sigmoid(x):
    return jax.nn.sigmoid(x)

def _layernorm(x, axis=-1, eps=1e-05):
    m = jnp.mean(x, axis=axis, keepdims=True)
    v = jnp.var(x, axis=axis, keepdims=True)
    return (x - m) / jnp.sqrt(v + eps)

def _scatter_add(tgt, idx, src, axis=0):
    return tgt.at[idx].add(src)

def _segment_sum(src, seg, n):
    return jax.ops.segment_sum(src, seg, n)
kernel_name = 'mk_adj_resnorm_d1_adj_r2_98479e'

def setup_inputs(seed: int=0):
    np.random.seed(seed)
    _w = jnp.asarray

    def _rec_inputs():
        import jax
        import jax.numpy as jnp
        _gk = jax.random.key(seed)
        x = 7.22e-05 + 1 * jax.random.normal(jax.random.fold_in(_gk, 1), (128, 64, 256), jnp.float32)
        _a = jax.random.bernoulli(jax.random.fold_in(_gk, 2), 0.125, (64, 64))
        adj = _a.astype(jnp.int32)
        return (x, adj)
    x, adj = _rec_inputs()

    def _L0_gnn_setup():
        import jax, jax.numpy as jnp
        import numpy as np
        LEAKY_ALPHA = 0.01
        NEG_INF = -1000000000.0
        LN_EPS = 1e-05

        def _gat_heads(x, adj, W, a):
            O = W.shape[-1]
            Wh = jnp.einsum('bnf,hfo->bhno', x, W)
            f1 = jnp.einsum('bhno,ho->bhn', Wh, a[:, :O])
            f2 = jnp.einsum('bhno,ho->bhn', Wh, a[:, O:])
            e = f1[:, :, :, None] + f2[:, :, None, :]
            e = jnp.where(e > 0, e, LEAKY_ALPHA * e)
            e = jnp.where(adj[None, None] > 0, e, NEG_INF)
            attn = jax.nn.softmax(e, axis=-1)
            return jnp.einsum('bhnm,bhmo->bhno', attn, Wh)
        key = jax.random.key(seed)
        ks = jax.random.split(key, 10)
        B, N, F_in, F_hid, H, F_out, D_ff = (8, 1024, 256, 256, 4, 256, 256)
        s = 0.05
        return {'enc_inputs': jax.random.normal(ks[0], (B, N, F_in), jnp.float32), 'adj': jax.random.randint(ks[1], (N, N), 0, 2, jnp.int32), 'W_heads': jax.random.normal(ks[2], (H, F_in, F_hid), jnp.float32) * s, 'a_heads': jax.random.normal(ks[3], (H, 2 * F_hid), jnp.float32) * s, 'W_out': jax.random.normal(ks[4], (H * F_hid, F_out), jnp.float32) * s, 'a_out': jax.random.normal(ks[5], (2 * F_out,), jnp.float32) * s, 'w1': jax.random.normal(ks[6], (F_out, D_ff), jnp.float32) * s, 'b1': jnp.zeros((D_ff,), jnp.float32), 'w2': jax.random.normal(ks[7], (D_ff, F_out), jnp.float32) * s, 'b2': jnp.zeros((F_out,), jnp.float32), 'ln_gamma': jnp.ones((F_out,), jnp.float32), 'ln_beta': jnp.zeros((F_out,), jnp.float32)}
    _L0_gnn_all = _L0_gnn_setup()
    _L0_gnn_in = {k: v for k, v in _L0_gnn_all.items() if k in ('W_heads', 'a_heads', 'W_out', 'a_out', 'w1', 'b1', 'w2', 'b2', 'ln_gamma', 'ln_beta')}
    del _L0_gnn_all
    return {'x': x, 'adj': adj, 'L0_gnn_W_heads': _L0_gnn_in['W_heads'], 'L0_gnn_a_heads': _L0_gnn_in['a_heads'], 'L0_gnn_W_out': _L0_gnn_in['W_out'], 'L0_gnn_a_out': _L0_gnn_in['a_out'], 'L0_gnn_w1': _L0_gnn_in['w1'], 'L0_gnn_b1': _L0_gnn_in['b1'], 'L0_gnn_w2': _L0_gnn_in['w2'], 'L0_gnn_b2': _L0_gnn_in['b2'], 'L0_gnn_ln_gamma': _L0_gnn_in['ln_gamma'], 'L0_gnn_ln_beta': _L0_gnn_in['ln_beta']}

def reference(x, adj, L0_gnn_W_heads, L0_gnn_a_heads, L0_gnn_W_out, L0_gnn_a_out, L0_gnn_w1, L0_gnn_b1, L0_gnn_w2, L0_gnn_b2, L0_gnn_ln_gamma, L0_gnn_ln_beta):
    import jax
    import jax.numpy as jnp

    def _L0_gnn_ref(enc_inputs, adj, W_heads, a_heads, W_out, a_out, w1, b1, w2, b2, ln_gamma, ln_beta):
        import jax, jax.numpy as jnp
        import numpy as np
        LEAKY_ALPHA = 0.01
        NEG_INF = -1000000000.0
        LN_EPS = 1e-05

        def _gat_heads(x, adj, W, a):
            O = W.shape[-1]
            Wh = jnp.einsum('bnf,hfo->bhno', x, W)
            f1 = jnp.einsum('bhno,ho->bhn', Wh, a[:, :O])
            f2 = jnp.einsum('bhno,ho->bhn', Wh, a[:, O:])
            e = f1[:, :, :, None] + f2[:, :, None, :]
            e = jnp.where(e > 0, e, LEAKY_ALPHA * e)
            e = jnp.where(adj[None, None] > 0, e, NEG_INF)
            attn = jax.nn.softmax(e, axis=-1)
            return jnp.einsum('bhnm,bhmo->bhno', attn, Wh)
        B, N, _ = enc_inputs.shape
        h = jax.nn.elu(_gat_heads(enc_inputs, adj, W_heads, a_heads))
        h = jnp.transpose(h, (0, 2, 1, 3)).reshape(B, N, -1)
        out = _gat_heads(h, adj, W_out[None], a_out[None])[:, 0]
        out = jax.nn.elu(out)
        ffn = jnp.maximum(out @ w1 + b1, 0.0) @ w2 + b2
        y = ffn + out
        mu = jnp.mean(y, axis=-1, keepdims=True)
        var = jnp.var(y, axis=-1, keepdims=True)
        return (y - mu) / jnp.sqrt(var + LN_EPS) * ln_gamma + ln_beta
    x = _layernorm(x + _L0_gnn_ref(x, adj, L0_gnn_W_heads, L0_gnn_a_heads, L0_gnn_W_out, L0_gnn_a_out, L0_gnn_w1, L0_gnn_b1, L0_gnn_w2, L0_gnn_b2, L0_gnn_ln_gamma, L0_gnn_ln_beta), axis=-1)
    return x

_drawn_inputs = setup_inputs


def setup_inputs(seed=0):
    import zlib

    import numpy as np

    out = dict(_drawn_inputs(seed))
    spreads = {'L0_gnn_b1': (0.0, 0.1),
     'L0_gnn_b2': (0.0, 0.1),
     'L0_gnn_ln_gamma': (1.0, 0.2),
     'L0_gnn_ln_beta': (0.0, 0.1)}
    factors = {}
    for name, (base, spread) in spreads.items():
        noise = np.random.default_rng([zlib.crc32(name.encode()), seed]).standard_normal(out[name].shape)
        drawn = base * np.exp(spread * noise) if base else spread * noise
        out[name] = jnp.asarray(drawn.astype(out[name].dtype))
    for name, factor in factors.items():
        out[name] = (out[name] * factor).astype(out[name].dtype)
    return out
```

```python
from contextlib import ExitStack

import numpy as np
import concourse.bass as bass
from concourse import mybir

F32 = mybir.dt.float32
F32R = mybir.dt.float32r
BF16 = mybir.dt.bfloat16
I32 = mybir.dt.int32
ALU = mybir.AluOpType
ACT = mybir.ActivationFunctionType
X = mybir.AxisListType.X

P = 128
T = 4
BIG = float(2.0 ** 100)
ALPHA = 0.01
EPS = 1e-5


def build(nc, x, adj, W_heads, a_heads, W_out, a_out, w1, b1, w2, b2, ln_gamma, ln_beta, out):
    B, N, F = x.shape
    HD, _, O = W_heads.shape
    FT, OT = F // P, O // P
    KT = HD * OT
    GROUPS = B * N // (P * T)
    ROWS = P * T
    WC = O + 2
    assert N * 2 == P and F == O == 256 and HD == 4

    x_rows = x.rearrange("b n f -> (b n) f")
    out_rows = out.rearrange("b n f -> (b n) f")

    def rows(ap, g):
        return ap[bass.ds(g * ROWS, ROWS), :].rearrange("(t p) f -> p t f", p=P)

    with ExitStack() as ctx:
        def sb(name, shape, dt=F32):
            return ctx.enter_context(nc.sbuf_tensor(name, [P] + shape, dt))[:]

        def sem(name):
            return ctx.enter_context(nc.semaphore(name))

        ident = sb("ident", [P])
        ident_r = sb("ident_r", [P], F32R)
        ident_b = sb("ident_b", [P], BF16)
        ident64 = sb("ident64", [N])
        block_ones = sb("block_ones", [P])
        ones_b = sb("ones_b", [P], BF16)
        adj_sb = sb("adj_sb", [N], I32)
        mask64 = sb("mask64", [N])
        mask_b = sb("mask_b", [HD, N], BF16)
        half = sb("half", [T])
        W_hi, W_lo = sb("W_hi", [FT, HD, O], F32R), sb("W_lo", [FT, HD, O], F32R)
        Wo_hi, Wo_lo = sb("Wo_hi", [KT, WC], F32R), sb("Wo_lo", [KT, WC], F32R)
        w1_hi, w1_lo = sb("w1_hi", [OT, O], F32R), sb("w1_lo", [OT, O], F32R)
        w2_hi, w2_lo = sb("w2_hi", [OT, O], F32R), sb("w2_lo", [OT, O], F32R)
        score_w = sb("score_w", [FT, 2, HD])
        b1_sb = sb("b1_sb", [OT])
        b2_rows = sb("b2_rows", [O], BF16)
        gamma_sb, beta_sb = sb("gamma_sb", [O]), sb("beta_sb", [O])

        x_sb = sb("x_sb", [T, F])
        x_hi, x_lo = sb("x_hi", [T, F], F32R), sb("x_lo", [T, F], F32R)
        f12 = sb("f12", [2, T, HD])
        score_work = sb("score_work", [2, T * HD * N])
        diag, e1 = (score_work[:, i].rearrange("p (t h m) -> p t h m", t=T, h=HD) for i in range(2))
        xT = score_work[:, 1].rearrange("p (f n) -> p f n", f=FT)
        mx1, ml1, z1 = sb("mx1", [T, HD]), sb("ml1", [T, HD]), sb("z1", [T, HD])
        att1 = sb("att1", [T, HD, P])
        att1T_hi, att1T_lo = sb("att1T_hi", [T, HD, P], F32R), sb("att1T_lo", [T, HD, P], F32R)
        Y_hi, Y_lo = sb("Y_hi", [FT, HD, T, P], F32R), sb("Y_lo", [FT, HD, T, P], F32R)
        h_work = sb("h_work", [max(2 * OT * ROWS, KT * WC)])
        h_exp, h_full = (h_work[:, i * OT * ROWS:(i + 1) * OT * ROWS].rearrange("p (o n) -> p o n", o=OT) for i in range(2))
        h_hi, h_lo = sb("h_hi", [HD, OT, ROWS], F32R), sb("h_lo", [HD, OT, ROWS], F32R)
        wh_hi, wh_lo = sb("wh_hi", [T, O], F32R), sb("wh_lo", [T, O], F32R)
        g12 = sb("g12", [T, 2])
        diag2 = sb("diag2", [T, N])
        e2 = sb("e2", [T, N])
        mx2, ml2, z2 = sb("mx2", [T]), sb("ml2", [T]), sb("z2", [T])
        att2 = sb("att2", [T, P])
        att2T_hi, att2T_lo = sb("att2T_hi", [T, P], F32R), sb("att2T_lo", [T, P], F32R)
        o_work = sb("o_work", [2, OT, ROWS])
        o_exp, o_full = o_work[:, 0], o_work[:, 1]
        o_hi, o_lo = sb("o_hi", [OT, ROWS], F32R), sb("o_lo", [OT, ROWS], F32R)
        h1_full = o_full
        h1_hi, h1_lo = (a.rearrange("p t h n -> p (t h n)")[:, 0:OT * ROWS].rearrange("p (o n) -> p o n", o=OT)
                        for a in (att1T_hi, att1T_lo))
        spare = sb("spare", [1])
        st1, mv1 = sb("st1", [T, 6]), sb("mv1", [T, 2])
        rs1, nm1, ve1 = sb("rs1", [T]), sb("nm1", [T]), sb("ve1", [T])
        st2, mv2 = sb("st2", [T, 6]), sb("mv2", [T, 2])
        rs2, nm2, ve2 = sb("rs2", [T]), sb("nm2", [T]), sb("ve2", [T])
        tail_work = sb("tail_work", [2, T, O])
        yn, res = tail_work[:, 0], tail_work[:, 1]
        xr = sb("xr", [T, F])

        a_sb = score_work.rearrange("p i (h w o) -> p (i h) w o", w=2, o=O)
        Wh_raw = o_work.rearrange("p a o n -> p (a o n)").rearrange("p (t h o) -> p t h o", t=FT, h=HD)
        Wo_raw = h_work[:, 0:KT * WC].rearrange("p (k c) -> p k c", c=WC)
        prod = res
        w12_raw = yn.rearrange("p (i k) o -> p i k o", i=2)
        ao_sb, b2_sb, b2_r = xr[:, 0:2], xr[:, 2], xr[:, 3]
        b2_p = res.rearrange("p t o -> p (t o)").bitcast(BF16)[:, 0:3 * O].rearrange("p (i o) -> p i o", i=3)

        heavy = [ctx.enter_context(nc.psum_tensor(f"heavy{i}", [P, 2, 512], F32))[:] for i in range(2)]
        light = [ctx.enter_context(nc.psum_tensor(f"light{i}", [P, 2, 512], F32))[:] for i in range(2)]

        def tiles(ap, c):
            return ap.rearrange("p b (u c) -> p (b u) c", c=c)

        s_load = sem("s_load")
        s_const = sem("s_const")
        s_setup = sem("s_setup")
        s_weights = sem("s_weights")
        s_front = sem("s_front")
        s_wcopy = sem("s_wcopy")
        x_loaded = sem("x_loaded")
        xh_done, x_split = sem("xh_done"), sem("x_split")
        xt_done, xt_out = sem("xt_done"), sem("xt_out")
        f_done, f_out = sem("f_done"), sem("f_out")
        diag_ready = sem("diag_ready")
        s_done, sm1, exp1 = sem("s_done"), sem("sm1"), sem("exp1")
        pt_done, pt_hi, pt_lo = sem("pt_done"), sem("pt_hi"), sem("pt_lo")
        y_done, y_hi, y_lo = sem("y_done"), sem("y_hi"), sem("y_lo")
        h_done, h_expd, h_elu = sem("h_done"), sem("h_expd"), sem("h_elu")
        h_min = sem("h_min")
        hh_done, hl_done = sem("hh_done"), sem("hl_done")
        w_done, w_hi_s, w_lo_s = sem("w_done"), sem("w_hi_s"), sem("w_lo_s")
        g12_out, diag2_ready = sem("g12_out"), sem("diag2_ready")
        s2_done, sm2, exp2 = sem("s2_done"), sem("sm2"), sem("exp2")
        pt2_done, pt2_hi, pt2_lo = sem("pt2_done"), sem("pt2_hi"), sem("pt2_lo")
        o_done, o_expd, o_min, o_elu = sem("o_done"), sem("o_expd"), sem("o_min"), sem("o_elu")
        oh_done, ol_done = sem("oh_done"), sem("ol_done")
        h1_done, h1_relu = sem("h1_done"), sem("h1_relu")
        h1h_done, h1l_done = sem("h1h_done"), sem("h1l_done")
        ff_done = sem("ff_done")
        ln1, ln1_pow, ln1_norm = sem("ln1"), sem("ln1_pow"), sem("ln1_norm")
        xr_loaded, resid = sem("xr_loaded"), sem("resid")
        ln2, ln2_pow, ln2_norm = sem("ln2"), sem("ln2_pow"), sem("ln2_norm")
        stored = sem("stored")

        block = ctx.enter_context(nc.Block())
        LAST = GROUPS - 1
        LOADS = 0

        def has(g):
            return not isinstance(g, int) or 0 <= g <= LAST

        def later(g):
            return not isinstance(g, int) or g > 0

        def periods(eng, period):
            for p in range(-2, 3):
                period(p)
            with eng.Fori(3, GROUPS - 2) as p:
                period(p)
            for p in range(GROUPS - 2, GROUPS + 2):
                period(p)

        N_LOADS = 13

        @block.sync
        def _(sp):
            sp.dma_start(a_sb, a_heads.rearrange("h (w o) -> h w o", w=2).partition_broadcast(P)).then_inc(s_load, 16)
            for ft in range(FT):
                sp.dma_start(Wh_raw[:, ft], W_heads[:, ft * P:(ft + 1) * P, :].rearrange("h p o -> p h o")).then_inc(s_load, 16)
            for b in range(2):
                sp.dma_start(adj_sb[b * N:(b + 1) * N], adj).then_inc(s_load, 16)
            sp.dma_start(ao_sb, a_out.rearrange("(w o) -> w o", w=2).partition_broadcast(P)).then_inc(s_load, 16)
            sp.dma_start(Wo_raw[:, :, 0:O], W_out.rearrange("(k p) o -> p k o", p=P)).then_inc(s_load, 16)
            for i, w in enumerate((w1, w2)):
                sp.dma_start(w12_raw[:, i], w.rearrange("(k p) o -> p k o", p=P)).then_inc(s_load, 16)
            sp.dma_start(b1_sb, b1.rearrange("(t p) -> p t", p=P), allow_slow_non_contiguous=True).then_inc(s_load, 16)
            for dst, src in ((b2_sb, b2), (gamma_sb, ln_gamma), (beta_sb, ln_beta)):
                sp.dma_start(dst, src.partition_broadcast(P)).then_inc(s_load, 16)

            def load_x(g):
                if not has(g):
                    return
                if later(g):
                    sp.wait_ge(x_split, g)
                    sp.wait_ge(xt_done, g)
                sp.dma_start(x_sb, rows(x_rows, g)).then_inc(x_loaded, 16)

            def load_xr(g):
                if not has(g):
                    return
                if later(g):
                    sp.wait_ge(resid, 3 * g)
                else:
                    sp.wait_ge(s_weights, 1)
                sp.dma_start(xr, rows(x_rows, g)).then_inc(xr_loaded, 16)

            def store(g):
                if not has(g):
                    return
                sp.wait_ge(ln2_norm, g + 1)
                sp.dma_start(rows(out_rows, g), res).then_inc(stored, 16)

            def period(p):
                load_x(p + 2)
                store(p - 2)
                load_xr(p - 1)
            periods(sp, period)
            sp.wait_ge(stored, 16 * GROUPS)

        @block.gpsimd
        def _(pool):
            g_ = nc.gpsimd
            g_.memset(ident, 0.0).then_inc(s_const, 1)
            pool.wait_ge(s_const, 1)
            g_.affine_select(out=ident, in_=ident, compare_op=ALU.not_equal, fill=1.0, base=0,
                             pattern=[[-1, P]], channel_multiplier=1).then_inc(s_const, 1)
            pool.wait_ge(s_front, 1)

            def split_x(g):
                if not has(g):
                    return
                if later(g):
                    pool.wait_ge(y_done, 4 * g)
                pool.wait_ge(xh_done, g + 1)
                g_.tensor_sub(x_lo, x_sb, x_hi.bitcast(F32)).then_inc(x_split, 1)

            def spread_f2(g):
                if not has(g):
                    return
                pool.wait_ge(f_out, g + 1)
                if later(g):
                    pool.wait_ge(s_done, g)
                g_.tensor_mul(diag.rearrange("p t h m -> p (t h) m"),
                              ident64.unsqueeze(1).broadcast_to([P, T * HD, N]),
                              f12[:, 1].rearrange("p t h -> p (t h)").unsqueeze(2).broadcast_to([P, T * HD, N])
                              ).then_inc(diag_ready, 1)

            def spread_g2(g):
                if not has(g):
                    return
                pool.wait_ge(g12_out, 2 * (g + 1))
                if later(g):
                    pool.wait_ge(s2_done, g)
                g_.tensor_mul(diag2, ident64.unsqueeze(1).broadcast_to([P, T, N]),
                              g12[:, :, 1:2].broadcast_to([P, T, N])).then_inc(diag2_ready, 1)

            def h_low(g, h):
                if not has(g):
                    return
                if h == 0 and later(g):
                    pool.wait_ge(w_done, 2 * g)
                pool.wait_ge(h_elu, 4 * g + h + 1)
                pool.wait_ge(hh_done, 4 * g + h + 1)
                g_.tensor_sub(h_lo[:, h], h_full, h_hi[:, h].bitcast(F32)).then_inc(hl_done, 1)

            def o_low(g):
                if not has(g):
                    return
                if later(g):
                    pool.wait_ge(ff_done, g)
                pool.wait_ge(o_elu, g + 1)
                pool.wait_ge(oh_done, g + 1)
                g_.tensor_sub(o_lo, o_full, o_hi.bitcast(F32)).then_inc(ol_done, 1)

            def inverse_root(g, ln, mv_eps, rs, done):
                if not has(g):
                    return
                pool.wait_ge(ln, 4 * g + 3)
                g_.tensor_tensor(rs, mv_eps, half, ALU.pow).then_inc(done, 1)

            def residual(g):
                if not has(g):
                    return
                pool.wait_ge(xr_loaded, 16 * (g + 1))
                g_.tensor_add(xr, xr, beta_sb.unsqueeze(1).broadcast_to([P, T, O])).then_inc(resid, 1)
                pool.wait_ge(ln1_norm, g + 1)
                g_.tensor_mul(yn, yn, gamma_sb.unsqueeze(1).broadcast_to([P, T, O])).then_inc(resid, 1)
                pool.wait_ge(resid, 3 * g + 2)
                if later(g):
                    pool.wait_ge(stored, 16 * g)
                g_.tensor_add(res, yn, xr).then_inc(resid, 1)

            def period(p):
                spread_g2(p - 1)
                h_low(p, 0)
                residual(p - 2)
                h_low(p, 1)
                inverse_root(p - 2, ln2, ve2, rs2, ln2_pow)
                h_low(p, 2)
                h_low(p, 3)
                spread_f2(p + 2)
                o_low(p - 1)
                split_x(p + 2)
                inverse_root(p - 1, ln1, ve1, rs1, ln1_pow)
            periods(pool, period)

        @block.scalar
        def _(act):
            s_ = nc.scalar

            def copy(dst, src):
                return s_.activation(dst, src, ACT.Copy)

            act.wait_ge(s_load, 16 * N_LOADS)
            copy(W_hi, Wh_raw).then_inc(s_wcopy, 1)
            copy(w1_hi, w12_raw[:, 0]).then_inc(s_wcopy, 1)
            copy(w2_hi, w12_raw[:, 1]).then_inc(s_wcopy, 1)

            def x_high(g):
                if not has(g):
                    return
                if later(g):
                    act.wait_ge(y_done, 4 * g)
                act.wait_ge(x_loaded, 16 * (g + 1))
                copy(x_hi, x_sb).then_inc(xh_done, 1)

            def xt_copy(g):
                if not has(g):
                    return
                act.wait_ge(xt_done, g + 1)
                if later(g):
                    act.wait_ge(f_done, g)
                copy(xT, light[0]).then_inc(xt_out, 1)

            def exp_1(g):
                if not has(g):
                    return
                act.wait_ge(sm1, 9 * g + 6)
                s_.activation(e1, e1, ACT.Exp).then_inc(exp1, 1)

            def exp_2(g):
                if not has(g):
                    return
                act.wait_ge(sm2, 9 * g + 6)
                s_.activation(e2, e2, ACT.Exp).then_inc(exp2, 1)

            def pt_high(g, u):
                if not has(g):
                    return
                act.wait_ge(pt_done, 2 * g + u + 1)
                if u == 0 and later(g):
                    act.wait_ge(y_done, 4 * g)
                copy(att1T_hi[:, 2 * u:2 * u + 2].rearrange("p t h n -> p t (h n)"), light[u]).then_inc(pt_hi, 1)

            def y_high(g, t):
                if not has(g):
                    return
                act.wait_ge(y_done, 4 * g + t + 1)
                if t == 0 and later(g):
                    act.wait_ge(h_done, 4 * g)
                copy(Y_hi[:, :, :, t].rearrange("p f h n -> p (f h) n"),
                     heavy[t % 2].rearrange("p f (h n) -> p (f h) n", n=P)).then_inc(y_hi, 1)

            def h_exps(g, h):
                if not has(g):
                    return
                act.wait_ge(h_done, 4 * g + h + 1)
                if h > 0 or later(g):
                    act.wait_ge(h_elu, 4 * g + h)
                s_.activation(h_exp, heavy[h % 2], ACT.Exp).then_inc(h_expd, 1)

            def h_high(g, h):
                if not has(g):
                    return
                act.wait_ge(h_elu, 4 * g + h + 1)
                if h == 0 and later(g):
                    act.wait_ge(w_done, 2 * g)
                copy(h_hi[:, h], h_full).then_inc(hh_done, 1)

            def w_high(g, u):
                if not has(g):
                    return
                act.wait_ge(w_done, 2 * g + u + 1)
                if u == 0 and later(g):
                    act.wait_ge(o_done, g)
                copy(wh_hi[:, 2 * u:2 * u + 2], heavy[u][:, :, 0:O]).then_inc(w_hi_s, 1)

            def pt2_high(g):
                if not has(g):
                    return
                act.wait_ge(pt2_done, g + 1)
                if later(g):
                    act.wait_ge(o_done, g)
                copy(att2T_hi.rearrange("p t n -> p (t n)"), light[1][:, 0]).then_inc(pt2_hi, 1)

            def o_exps(g):
                if not has(g):
                    return
                act.wait_ge(o_done, g + 1)
                if later(g):
                    act.wait_ge(o_elu, g)
                s_.activation(o_exp, light[1], ACT.Exp).then_inc(o_expd, 1)

            def o_high(g):
                if not has(g):
                    return
                act.wait_ge(o_elu, g + 1)
                if later(g):
                    act.wait_ge(ff_done, g)
                copy(o_hi, o_full).then_inc(oh_done, 1)

            def h1_act(g):
                if not has(g):
                    return
                act.wait_ge(h1_done, g + 1)
                if later(g):
                    act.wait_ge(h1l_done, g)
                s_.activation(h1_full[:, 0], light[1][:, 0], ACT.Relu, bias=b1_sb[:, 0:1])
                s_.activation(h1_full[:, 1], light[1][:, 1], ACT.Relu, bias=b1_sb[:, 1:2]).then_inc(h1_relu, 1)
                act.wait_ge(h1_relu, g + 1)
                if later(g):
                    act.wait_ge(ff_done, g)
                copy(h1_hi, h1_full).then_inc(h1h_done, 1)

            def norm(dst, src, rs, nm, done):
                for t in range(T):
                    last = s_.activation(dst[:, t], src[:, t], ACT.Identity, bias=nm[:, t:t + 1], scale=rs[:, t:t + 1])
                last.then_inc(done, 1)

            def norm_1(g):
                if not has(g):
                    return
                act.wait_ge(ln1, 4 * g + 4)
                if later(g):
                    act.wait_ge(resid, 3 * g)
                norm(yn, tiles(light[1], O), rs1, nm1, ln1_norm)

            def norm_2(g):
                if not has(g):
                    return
                act.wait_ge(ln2, 4 * g + 4)
                norm(res, res, rs2, nm2, ln2_norm)

            def period(p):
                h_exps(p, 0)
                h_high(p, 0)
                exp_2(p - 1)
                h_exps(p, 1)
                h_high(p, 1)
                h_exps(p, 2)
                h_high(p, 2)
                pt_high(p + 1, 0)
                pt_high(p + 1, 1)
                h_exps(p, 3)
                h_high(p, 3)
                norm_2(p - 2)
                xt_copy(p + 2)
                pt2_high(p - 1)
                y_high(p + 1, 0)
                y_high(p + 1, 1)
                o_exps(p - 1)
                y_high(p + 1, 2)
                o_high(p - 1)
                y_high(p + 1, 3)
                x_high(p + 2)
                exp_1(p + 2)
                w_high(p, 0)
                h1_act(p - 1)
                w_high(p, 1)
                norm_1(p - 1)
            periods(act, period)

        @block.vector
        def _(dve):
            v_ = nc.vector
            setup = [0]

            def link(ins):
                setup[0] += 1
                ins.then_inc(s_setup, 1)
                dve.wait_ge(s_setup, setup[0])

            v_.memset(half, -0.5)
            v_.memset(ones_b, 1.0)
            v_.memset(att1, 0.0)
            v_.memset(att2, 0.0)
            v_.memset(b2_rows, 0.0)
            link(v_.memset(block_ones, 0.0))
            v_.memset(block_ones[0:N, 0:N], 1.0)
            v_.memset(block_ones[N:P, N:P], 1.0)
            dve.wait_ge(s_const, 2)
            dve.wait_ge(s_load, 16 * N_LOADS)
            v_.tensor_copy(ident_r, ident)
            v_.tensor_copy(ident_b, ident)
            v_.tensor_scalar(mask64, adj_sb, 0.0, BIG, ALU.is_gt, ALU.mult)
            link(v_.tensor_add(ident64, ident[:, 0:N], ident[:, N:P]))
            v_.tensor_scalar(mask_b, mask64.unsqueeze(1).broadcast_to([P, HD, N]), -BIG, None, ALU.add)
            for ft in range(FT):
                for w in range(2):
                    link(v_.tensor_mul(prod, Wh_raw[:, ft], a_sb[:, :, w]))
                    link(v_.reduce_sum(score_w[:, ft, w], prod, axis=X))
            v_.engine_nop().then_inc(s_front, 1)
            for w in range(2):
                for k in range(0, KT, T):
                    link(v_.tensor_mul(prod, Wo_raw[:, k:k + T, 0:O], ao_sb[:, w:w + 1].broadcast_to([P, T, O])))
                    link(v_.reduce_sum(Wo_raw[:, k:k + T, O + w:O + w + 1].rearrange("p k c -> p (k c)"), prod, axis=X))
            link(v_.tensor_copy(Wo_hi, Wo_raw))
            v_.tensor_sub(Wo_lo, Wo_raw, Wo_hi.bitcast(F32))
            link(v_.tensor_copy(b2_p[:, 0], b2_sb))
            link(v_.tensor_sub(b2_r, b2_sb, b2_p[:, 0]))
            link(v_.tensor_copy(b2_p[:, 1], b2_r))
            link(v_.tensor_sub(b2_r, b2_r, b2_p[:, 1]))
            link(v_.tensor_copy(b2_p[:, 2], b2_r))
            for i in range(3):
                v_.tensor_copy(b2_rows[32 * i:32 * i + 1], b2_p[32 * i:32 * i + 1, i])
            dve.wait_ge(s_wcopy, 3)
            v_.tensor_sub(W_lo, Wh_raw, W_hi.bitcast(F32))
            v_.tensor_sub(w1_lo, w12_raw[:, 0], w1_hi.bitcast(F32))
            v_.tensor_sub(w2_lo, w12_raw[:, 1], w2_hi.bitcast(F32)).then_inc(s_weights, 1)

            def f_copy(g):
                if not has(g):
                    return
                dve.wait_ge(f_done, g + 1)
                if later(g):
                    dve.wait_ge(diag_ready, g)
                v_.tensor_copy(f12, light[0][:, 0, 0:T * 2 * HD].rearrange("p (t w h) -> p w t h", w=2, h=HD)
                               ).then_inc(f_out, 1)

            def scores(g, done, sm, psum, own, e, mx, ml, read):
                dve.wait_ge(done, g + 1)
                if later(g):
                    dve.wait_ge(read, g)
                J = e.shape[1]
                own_b = own.unsqueeze(2).broadcast_to([P, J, N])
                v_.reduce_max(mx, psum, axis=X).then_inc(sm, 1)
                v_.tensor_add(e, psum, own_b).then_inc(sm, 1)
                dve.wait_ge(sm, 9 * g + 1)
                v_.tensor_add(mx, mx, own).then_inc(sm, 1)
                dve.wait_ge(sm, 9 * g + 2)
                v_.scalar_tensor_tensor(e, e, ALPHA, e, ALU.mult, ALU.max).then_inc(sm, 1)
                dve.wait_ge(sm, 9 * g + 3)
                v_.scalar_tensor_tensor(ml, mx, ALPHA, mx, ALU.mult, ALU.max).then_inc(sm, 1)
                dve.wait_ge(sm, 9 * g + 5)
                v_.tensor_sub(e, e, ml.unsqueeze(2).broadcast_to([P, J, N])).then_inc(sm, 1)

            def softmax(g, exp, sm, e, z, att, transposed, n):
                dve.wait_ge(exp, g + 1)
                J = e.shape[1]
                v_.reduce_sum(z, e, axis=X).then_inc(sm, 1)
                dve.wait_ge(sm, 9 * g + 7)
                v_.reciprocal(z, z).then_inc(sm, 1)
                dve.wait_ge(sm, 9 * g + 8)
                if later(g):
                    dve.wait_ge(transposed, n * g)
                for b in range(2):
                    s = slice(b * N, (b + 1) * N)
                    last = v_.tensor_mul(att[s, :, s], e[s], z[s].unsqueeze(2).broadcast_to([N, J, N]))
                last.then_inc(sm, 1)

            def flat(ap):
                return ap.rearrange("p t h m -> p (t h) m")

            def row(ap):
                return ap.rearrange("p t h -> p (t h)")

            def scores_1(g):
                if has(g):
                    scores(g, s_done, sm1, tiles(light[0], HD * N).rearrange("p t (h m) -> p (t h) m", m=N),
                           row(f12[:, 0]), flat(e1), row(mx1), row(ml1), sm1_used(g))

            def sm1_used(g):
                return exp1

            def softmax_1(g):
                if has(g):
                    softmax(g, exp1, sm1, flat(e1), row(z1), flat(att1), pt_done, 2)

            def scores_2(g):
                if has(g):
                    scores(g, s2_done, sm2, light[1][:, 0, 0:T * N].rearrange("p (t m) -> p t m", m=N),
                           g12[:, :, 0:1].rearrange("p t c -> p (t c)"), e2, mx2, ml2, exp2)

            def softmax_2(g):
                if has(g):
                    softmax(g, exp2, sm2, e2, z2, att2, pt2_done, 1)

            def pt_low(g, u):
                if not has(g):
                    return
                dve.wait_ge(pt_hi, 2 * g + u + 1)
                if u == 0 and later(g):
                    dve.wait_ge(y_done, 4 * g)
                hi, lo = ((a[:, 2 * u:2 * u + 2].rearrange("p t h n -> p t (h n)")) for a in (att1T_hi, att1T_lo))
                v_.tensor_sub(lo, light[u], hi.bitcast(F32)).then_inc(pt_lo, 1)

            def y_low(g, t):
                if not has(g):
                    return
                dve.wait_ge(y_hi, 4 * g + t + 1)
                if t == 0 and later(g):
                    dve.wait_ge(h_done, 4 * g)
                hi, lo = (a[:, :, :, t].rearrange("p f h n -> p (f h) n") for a in (Y_hi, Y_lo))
                v_.tensor_sub(lo, heavy[t % 2].rearrange("p f (h n) -> p (f h) n", n=P), hi.bitcast(F32)
                              ).then_inc(y_lo, 1)

            def h_finish(g, h):
                if not has(g):
                    return
                dve.wait_ge(h_expd, 4 * g + h + 1)
                v_.tensor_scalar(h_exp, h_exp, 1.0, -1.0, ALU.min, ALU.add).then_inc(h_min, 1)
                dve.wait_ge(h_min, 4 * g + h + 1)
                if h > 0 or later(g):
                    dve.wait_ge(hl_done, 4 * g + h)
                v_.tensor_max(h_full, heavy[h % 2], h_exp).then_inc(h_elu, 1)

            def w_low(g, u):
                if not has(g):
                    return
                dve.wait_ge(w_hi_s, 2 * g + u + 1)
                if u == 0 and later(g):
                    dve.wait_ge(o_done, g)
                t = slice(2 * u, 2 * u + 2)
                v_.tensor_sub(wh_lo[:, t], heavy[u][:, :, 0:O], wh_hi[:, t].bitcast(F32)).then_inc(w_lo_s, 1)
                if u == 0 and later(g):
                    dve.wait_ge(diag2_ready, g)
                v_.tensor_copy(g12[:, t], heavy[u][:, :, O:WC]).then_inc(g12_out, 1)

            def pt2_low(g):
                if not has(g):
                    return
                dve.wait_ge(pt2_hi, g + 1)
                if later(g):
                    dve.wait_ge(o_done, g)
                v_.tensor_sub(att2T_lo.rearrange("p t n -> p (t n)"), light[1][:, 0],
                              att2T_hi.rearrange("p t n -> p (t n)").bitcast(F32)).then_inc(pt2_lo, 1)

            def o_finish(g):
                if not has(g):
                    return
                dve.wait_ge(o_expd, g + 1)
                v_.tensor_scalar(o_exp, o_exp, 1.0, -1.0, ALU.min, ALU.add).then_inc(o_min, 1)
                dve.wait_ge(o_min, g + 1)
                if later(g):
                    dve.wait_ge(ol_done, g)
                v_.tensor_max(o_full, light[1], o_exp).then_inc(o_elu, 1)

            def h1_low(g):
                if not has(g):
                    return
                dve.wait_ge(h1h_done, g + 1)
                if later(g):
                    dve.wait_ge(ff_done, g)
                v_.tensor_sub(h1_lo, h1_full, h1_hi.bitcast(F32)).then_inc(h1l_done, 1)

            def stats(g, ln, src, st, mv, ve):
                for t in range(T):
                    last = v_.bn_stats(st[:, t], src[:, t])
                last.then_inc(ln, 1)
                dve.wait_ge(ln, 4 * g + 1)
                v_.memset(spare, 0.0)
                for t in range(T):
                    last = v_.bn_aggr(mv[:, t], st[:, t])
                last.then_inc(ln, 1)
                dve.wait_ge(ln, 4 * g + 2)
                v_.tensor_scalar(ve.unsqueeze(2), mv[:, :, 1:2], EPS, None, ALU.add).then_inc(ln, 1)

            def shift(g, ln, pw, mv, rs, nm):
                dve.wait_ge(pw, g + 1)
                v_.scalar_tensor_tensor(nm.unsqueeze(2), mv[:, :, 0:1], -1.0, rs.unsqueeze(2), ALU.mult, ALU.mult
                                        ).then_inc(ln, 1)

            def stats_1(g):
                if has(g):
                    dve.wait_ge(ff_done, g + 1)
                    if later(g):
                        dve.wait_ge(ln1_norm, g)
                    stats(g, ln1, tiles(light[1], O), st1, mv1, ve1)

            def shift_1(g):
                if has(g):
                    shift(g, ln1, ln1_pow, mv1, rs1, nm1)

            def stats_2(g):
                if has(g):
                    dve.wait_ge(resid, 3 * g + 3)
                    if later(g):
                        dve.wait_ge(ln2_norm, g)
                    stats(g, ln2, res, st2, mv2, ve2)

            def shift_2(g):
                if has(g):
                    shift(g, ln2, ln2_pow, mv2, rs2, nm2)

            def period(p):
                scores_2(p - 1)
                h_finish(p, 0)
                softmax_2(p - 1)
                h_finish(p, 1)
                h_finish(p, 2)
                stats_2(p - 2)
                pt_low(p + 1, 0)
                pt_low(p + 1, 1)
                h_finish(p, 3)
                shift_2(p - 2)
                pt2_low(p - 1)
                y_low(p + 1, 0)
                f_copy(p + 2)
                y_low(p + 1, 1)
                o_finish(p - 1)
                y_low(p + 1, 2)
                y_low(p + 1, 3)
                scores_1(p + 2)
                w_low(p, 0)
                softmax_1(p + 2)
                h1_low(p - 1)
                w_low(p, 1)
                stats_1(p - 1)
                shift_1(p - 1)
            periods(dve, period)

        @block.tensor
        def _(pe):
            mm = nc.tensor.matmul

            def three(out_, pairs, first=True, last=True):
                n = len(pairs)
                for i, ((ahi, alo), (bhi, blo)) in enumerate(pairs):
                    mm(out_, ahi, bhi, start=first and i == 0, stop=False)
                    mm(out_, ahi, blo, start=False, stop=False)
                    ins = mm(out_, alo, bhi, start=False, stop=last and i == n - 1)
                return ins

            pe.wait_ge(s_front, 1)

            def x_transpose(g):
                if not has(g):
                    return
                pe.wait_ge(x_loaded, 16 * (g + 1))
                if later(g):
                    pe.wait_ge(sm1, 9 * (g - 1) + 2)
                if has(g - 1):
                    pe.wait_ge(pt_lo, 2 * (g - 1) + 1)
                for t in range(T):
                    for ft in range(FT):
                        ins = nc.tensor.transpose(light[0][:, ft, t * P:(t + 1) * P], x_sb[:, t, ft * P:(ft + 1) * P], ident)
                ins.then_inc(xt_done, 1)

            def score_terms(g):
                if not has(g):
                    return
                pe.wait_ge(xt_out, g + 1)
                for t in range(T):
                    for ft in range(FT):
                        ins = mm(light[0][:, 0, t * 2 * HD:(t + 1) * 2 * HD], xT[:, ft, t * P:(t + 1) * P],
                                 score_w[:, ft].rearrange("p w h -> p (w h)"), start=ft == 0, stop=ft == FT - 1)
                ins.then_inc(f_done, 1)

            def score_spread(g):
                if not has(g):
                    return
                pe.wait_ge(diag_ready, g + 1)
                ps = tiles(light[0], HD * N)
                for t in range(T):
                    mm(ps[:, t], ident_b, mask_b.rearrange("p h m -> p (h m)"), start=True, stop=False)
                    ins = mm(ps[:, t], block_ones, diag[:, t].rearrange("p h m -> p (h m)"), start=False, stop=True)
                ins.then_inc(s_done, 1)

            def att_transpose(g, u):
                if not has(g):
                    return
                if u == 0:
                    pe.wait_ge(sm1, 9 * g + 9)
                elif has(g - 2):
                    pe.wait_ge(sm2, 9 * (g - 2) + 2)
                for t in range(2 * u, 2 * u + 2):
                    for h in range(HD):
                        ins = nc.tensor.transpose(light[u][:, t - 2 * u, h * P:(h + 1) * P], att1[:, t, h], ident)
                ins.then_inc(pt_done, 1)

            def attend(g, t):
                if not has(g):
                    return
                pe.wait_ge(x_split, g + 1)
                pe.wait_ge(pt_lo, 2 * g + t // 2 + 1)
                if t < 2:
                    if has(g - 1):
                        pe.wait_ge(h_elu, 4 * (g - 1) + 3 + t)
                else:
                    pe.wait_ge(y_lo, 4 * g + t - 1)
                for ft in range(FT):
                    f = slice(ft * P, (ft + 1) * P)
                    ins = three(heavy[t % 2][:, ft], [((x_hi[:, t, f], x_lo[:, t, f]),
                                (att1T_hi[:, t].rearrange("p h n -> p (h n)"), att1T_lo[:, t].rearrange("p h n -> p (h n)")))])
                ins.then_inc(y_done, 1)

            def head(g, h):
                if not has(g):
                    return
                if h == 0:
                    pe.wait_ge(y_lo, 4 * g + 4)
                if h < 2:
                    if has(g - 1):
                        pe.wait_ge(g12_out, 2 * (g - 1) + h + 1)
                else:
                    pe.wait_ge(h_elu, 4 * g + h - 1)
                for ot in range(OT):
                    o = slice(ot * P, (ot + 1) * P)
                    ins = three(heavy[h % 2][:, ot],
                                [((W_hi[:, ft, h, o], W_lo[:, ft, h, o]),
                                  (Y_hi[:, ft, h].rearrange("p t n -> p (t n)"), Y_lo[:, ft, h].rearrange("p t n -> p (t n)")))
                                 for ft in range(FT)])
                ins.then_inc(h_done, 1)

            def project(g, u):
                if not has(g):
                    return
                if u == 0:
                    pe.wait_ge(hl_done, 4 * g + 4)
                if has(g + 1):
                    pe.wait_ge(y_lo, 4 * (g + 1) + 3 + u)
                else:
                    pe.wait_ge(h_elu, 4 * g + 3 + u)
                for t in range(2 * u, 2 * u + 2):
                    n = slice(t * P, (t + 1) * P)
                    ins = three(heavy[u][:, t - 2 * u, 0:WC],
                                [((h_hi[:, k // OT, k % OT, n], h_lo[:, k // OT, k % OT, n]), (Wo_hi[:, k], Wo_lo[:, k]))
                                 for k in range(KT)])
                ins.then_inc(w_done, 1)

            def score_spread_2(g):
                if not has(g):
                    return
                pe.wait_ge(diag2_ready, g + 1)
                if later(g):
                    pe.wait_ge(ln1_norm, g)
                for t in range(T):
                    mm(light[1][:, 0, t * N:(t + 1) * N], ident_b, mask_b[:, 0], start=True, stop=False)
                    ins = mm(light[1][:, 0, t * N:(t + 1) * N], block_ones, diag2[:, t], start=False, stop=True)
                ins.then_inc(s2_done, 1)

            def att2_transpose(g):
                if not has(g):
                    return
                pe.wait_ge(sm2, 9 * g + 9)
                if has(g + 2):
                    pe.wait_ge(pt_lo, 2 * (g + 2) + 2)
                for t in range(T):
                    ins = nc.tensor.transpose(light[1][:, 0, t * P:(t + 1) * P], att2[:, t], ident)
                ins.then_inc(pt2_done, 1)

            def attend_2(g):
                if not has(g):
                    return
                pe.wait_ge(pt2_lo, g + 1)
                pe.wait_ge(w_lo_s, 2 * g + 2)
                for t in range(T):
                    n = slice(t * P, (t + 1) * P)
                    for ot in range(OT):
                        o = slice(ot * P, (ot + 1) * P)
                        ins = three(light[1][:, ot, n], [((wh_hi[:, t, o], wh_lo[:, t, o]), (att2T_hi[:, t], att2T_lo[:, t]))])
                ins.then_inc(o_done, 1)

            def ffn_in(g):
                if not has(g):
                    return
                pe.wait_ge(ol_done, g + 1)
                for ft in range(OT):
                    f = slice(ft * P, (ft + 1) * P)
                    ins = three(light[1][:, ft], [((w1_hi[:, ot, f], w1_lo[:, ot, f]), (o_hi[:, ot], o_lo[:, ot]))
                                                  for ot in range(OT)])
                ins.then_inc(h1_done, 1)

            def ffn_out(g):
                if not has(g):
                    return
                pe.wait_ge(h1l_done, g + 1)
                ps = tiles(light[1], O)
                for t in range(T):
                    n = slice(t * P, (t + 1) * P)
                    mm(ps[:, t], ones_b, b2_rows, start=True, stop=False)
                    three(ps[:, t], [((h1_hi[:, ft, n], h1_lo[:, ft, n]), (w2_hi[:, ft], w2_lo[:, ft])) for ft in range(OT)],
                          first=False, last=False)
                    for ot in range(OT):
                        o = slice(ot * P, (ot + 1) * P)
                        mm(ps[:, t, o], o_hi[:, ot, n], ident_r, start=False, stop=False)
                        ins = mm(ps[:, t, o], o_lo[:, ot, n], ident_r, start=False, stop=ot == OT - 1)
                ins.then_inc(ff_done, 1)

            def period(p):
                if isinstance(p, int) and p == 0:
                    pe.wait_ge(s_weights, 1)
                head(p, 0)
                score_spread_2(p - 1)
                head(p, 1)
                head(p, 2)
                att_transpose(p + 1, 0)
                att_transpose(p + 1, 1)
                head(p, 3)
                x_transpose(p + 2)
                att2_transpose(p - 1)
                attend(p + 1, 0)
                attend(p + 1, 1)
                score_terms(p + 2)
                attend_2(p - 1)
                attend(p + 1, 2)
                attend(p + 1, 3)
                score_spread(p + 2)
                project(p, 0)
                ffn_in(p - 1)
                project(p, 1)
                ffn_out(p - 1)
            periods(pe, period)


INPUTS = ["x", "adj", "L0_gnn_W_heads", "L0_gnn_a_heads", "L0_gnn_W_out", "L0_gnn_a_out", "L0_gnn_w1", "L0_gnn_b1",
          "L0_gnn_w2", "L0_gnn_b2", "L0_gnn_ln_gamma", "L0_gnn_ln_beta"]


def kernel(**inputs):
    import numpy as _np
    import concourse.bacc as _bacc
    from concourse import mybir as _mybir
    from concourse.bass_utils import run_bass_kernel_spmd as _run

    nc = _bacc.Bacc("TRN2", target_bir_lowering=False, num_devices=1)
    arrays, args = {}, []
    for name in INPUTS:
        a = _np.ascontiguousarray(inputs[name])
        arrays[f"in_{name}"] = a
        args.append(nc.dram_tensor(f"in_{name}", a.shape, _mybir.dt.from_np(a.dtype), kind="ExternalInput").ap())
    shape = inputs["x"].shape
    args.append(nc.dram_tensor("out_0", shape, _mybir.dt.float32, kind="ExternalOutput").ap())
    build(nc, *args)
    return _run(nc, [arrays], core_ids=[0]).results[0]["out_0"]
```

```python
from contextlib import ExitStack

import numpy as np
import concourse.bass as bass
from concourse import mybir

F32 = mybir.dt.float32
F32R = mybir.dt.float32r
BF16 = mybir.dt.bfloat16
I32 = mybir.dt.int32
ALU = mybir.AluOpType
ACT = mybir.ActivationFunctionType
X = mybir.AxisListType.X

P = 128
T = 4
BIG = float(2.0 ** 100)
ALPHA = 0.01
EPS = 1e-5


def build(nc, x, adj, W_heads, a_heads, W_out, a_out, w1, b1, w2, b2, ln_gamma, ln_beta, out):
    B, N, F = x.shape
    HD, _, O = W_heads.shape
    FT, OT = F // P, O // P
    KT = HD * OT
    GROUPS = B * N // (P * T)
    ROWS = P * T
    WC = O + 2
    assert N * 2 == P and F == O == 256 and HD == 4

    x_rows = x.rearrange("b n f -> (b n) f")
    out_rows = out.rearrange("b n f -> (b n) f")

    def graphs(g):
        return x[bass.ds(g * 2 * T, 2 * T)].rearrange("b m f -> m b f")

    def rows(ap, g):
        return ap[bass.ds(g * ROWS, ROWS), :].rearrange("(t p) f -> p t f", p=P)

    with ExitStack() as ctx:
        def sb(name, shape, dt=F32):
            return ctx.enter_context(nc.sbuf_tensor(name, [P] + shape, dt))[:]

        def sem(name):
            return ctx.enter_context(nc.semaphore(name))

        ident = sb("ident", [P])
        ident_r = sb("ident_r", [P], F32R)
        ident_b = sb("ident_b", [P], BF16)
        ident64 = sb("ident64", [N])
        block_ones = sb("block_ones", [P], F32R)
        ones_b = sb("ones_b", [P], BF16)
        adj_sb = sb("adj_sb", [N], I32)
        mask64 = sb("mask64", [N])
        mask_b = sb("mask_b", [2, HD, N], BF16)
        half = sb("half", [T])
        W_hi, W_lo = sb("W_hi", [FT, HD, O], F32R), sb("W_lo", [FT, HD, O], F32R)
        Wo_hi, Wo_lo = sb("Wo_hi", [KT, WC], F32R), sb("Wo_lo", [KT, WC], F32R)
        w1_hi, w1_lo = sb("w1_hi", [OT, O], F32R), sb("w1_lo", [OT, O], F32R)
        w2_hi, w2_lo = sb("w2_hi", [OT, O], F32R), sb("w2_lo", [OT, O], F32R)
        score_w = sb("score_w", [FT, 2, HD])
        b1_sb = sb("b1_sb", [OT])
        b2_rows = sb("b2_rows", [O], BF16)
        gamma_sb, beta_sb = sb("gamma_sb", [O]), sb("beta_sb", [O])

        x_sb = sb("x_sb", [2 * T, F])
        x_split = sb("x_split", [2 * T, F], F32R)
        f12 = sb("f12", [2, T, HD])
        f2_hi, f2_lo = sb("f2_hi", [T, HD], F32R), sb("f2_lo", [T, HD])
        diag = sb("diag", [2, T, HD, N], F32R)
        score_work = sb("score_work", [3, T * HD * N])
        e1 = score_work[:, 0].rearrange("p (t h m) -> p t h m", t=T, h=HD)
        att1 = score_work[:, 1:3].rearrange("p i k -> p (i k)").rearrange("p (t h d m) -> p t h d m", t=T, h=HD, d=2)
        xT = score_work[:, 0].rearrange("p (f n) -> p f n", f=FT)
        mx1, ml1, z1 = sb("mx1", [T, HD]), sb("ml1", [T, HD]), sb("z1", [T, HD])
        att1T_hi, att1T_lo = sb("att1T_hi", [T, HD, P], F32R), sb("att1T_lo", [T, HD, P], F32R)
        Y_hi, Y_lo = sb("Y_hi", [FT, HD, T, P], F32R), sb("Y_lo", [FT, HD, T, P], F32R)
        h_work = sb("h_work", [max(2 * OT * ROWS, KT * WC)])
        h_full = [h_work[:, i * OT * ROWS:(i + 1) * OT * ROWS].rearrange("p (o n) -> p o n", o=OT) for i in range(2)]
        h_hi, h_lo = sb("h_hi", [HD, OT, ROWS], F32R), sb("h_lo", [HD, OT, ROWS], F32R)
        wh_hi, wh_lo = sb("wh_hi", [T, O], F32R), sb("wh_lo", [T, O], F32R)
        g12 = sb("g12", [T, 2])
        g2_hi, g2_lo = sb("g2_hi", [T], F32R), sb("g2_lo", [T])
        diag2 = diag.rearrange("p i t h m -> p (i t h m)")[:, 0:2 * T * N].rearrange("p (i t m) -> p i t m", i=2, t=T)
        e2 = score_work[:, 0, 0:T * N].rearrange("p (t m) -> p t m", m=N)
        mx2, ml2, z2 = sb("mx2", [T]), sb("ml2", [T]), sb("z2", [T])
        att2 = sb("att2", [T, P])
        att2T_hi, att2T_lo = sb("att2T_hi", [T, P], F32R), sb("att2T_lo", [T, P], F32R)
        o_full = sb("o_full", [OT, ROWS])
        h1_full = o_full
        o_hi, o_lo = sb("o_hi", [OT, ROWS], F32R), sb("o_lo", [OT, ROWS], F32R)
        h1_hi, h1_lo = (a.rearrange("p t h n -> p (t h n)")[:, 0:OT * ROWS].rearrange("p (o n) -> p o n", o=OT)
                        for a in (att1T_hi, att1T_lo))
        spare = sb("spare", [1])
        st1, mv1 = sb("st1", [T, 6]), sb("mv1", [T, 2])
        rs1, nm1, ve1 = sb("rs1", [T]), sb("nm1", [T]), sb("ve1", [T])
        st2, mv2 = sb("st2", [T, 6]), sb("mv2", [T, 2])
        rs2, nm2, ve2 = sb("rs2", [T]), sb("nm2", [T]), sb("ve2", [T])
        yn = sb("yn", [T, O])
        xr = sb("xr", [T, F])

        a_sb = score_work[:, 0:2].rearrange("p i (h w o) -> p (i h) w o", w=2, o=O)
        Wh_raw = [yn, o_full.rearrange("p o n -> p (o n)").rearrange("p (h o) -> p h o", h=HD)]
        Wo_raw = h_work[:, 0:KT * WC].rearrange("p (k c) -> p k c", c=WC)
        w12_raw = yn.rearrange("p (i k) o -> p i k o", i=2)
        ao_sb, b2_sb, b2_r = xr[:, 0:2], xr[:, 2], xr[:, 3]
        b2_p = sb("b2_p", [O], BF16)

        heavy = [ctx.enter_context(nc.psum_tensor(f"heavy{i}", [P, 2, 512], F32))[:] for i in range(2)]
        light = [ctx.enter_context(nc.psum_tensor(f"light{i}", [P, 2, 512], F32))[:] for i in range(2)]

        product = [heavy[i // 4].rearrange("p b (c o) -> p (b c) o", o=O)[:, i % 4] for i in range(8)]

        def tiles(ap, c):
            return ap.rearrange("p b (u c) -> p (b u) c", c=c)

        s_load_front, s_load = sem("s_load_front"), sem("s_load")
        s_load_w12 = sem("s_load_w12")
        s_adj = sem("s_adj")
        s_const = sem("s_const")
        s_setup = sem("s_setup")
        s_front = sem("s_front")
        s_wo = sem("s_wo")
        s_wcopy = sem("s_wcopy")
        s_weights = sem("s_weights")
        s_b2 = sem("s_b2")
        x_loaded = sem("x_loaded")
        xh_done, xs_done = sem("xh_done"), sem("xs_done")
        xt_done, xt_out = sem("xt_done"), sem("xt_out")
        f_done, f_out = sem("f_done"), sem("f_out")
        diag_ready = sem("diag_ready")
        s_done, sm1, exp1 = sem("s_done"), sem("sm1"), sem("exp1")
        att_twice = sem("att_twice")
        pt_done, pt_hi, pt_lo = sem("pt_done"), sem("pt_hi"), sem("pt_lo")
        y_done, y_hi, y_lo = sem("y_done"), sem("y_hi"), sem("y_lo")
        h_done, h_expd, h_elu = sem("h_done"), sem("h_expd"), sem("h_elu")
        h_min = sem("h_min")
        hh_done, hl_done = sem("hh_done"), sem("hl_done")
        w_done, w_hi_s, w_lo_s = sem("w_done"), sem("w_hi_s"), sem("w_lo_s")
        g12_out, diag2_ready = sem("g12_out"), sem("diag2_ready")
        s2_done, sm2, exp2 = sem("s2_done"), sem("sm2"), sem("exp2")
        pt2_done, pt2_hi, pt2_lo = sem("pt2_done"), sem("pt2_hi"), sem("pt2_lo")
        o_done, o_expd, o_min, o_elu = sem("o_done"), sem("o_expd"), sem("o_min"), sem("o_elu")
        oh_done, ol_done = sem("oh_done"), sem("ol_done")
        h1_done, h1_relu = sem("h1_done"), sem("h1_relu")
        h1h_done, h1l_done = sem("h1h_done"), sem("h1l_done")
        ff_done = sem("ff_done")
        ln1, ln1_pow, ln1_norm = sem("ln1"), sem("ln1_pow"), sem("ln1_norm")
        xr_loaded, resid = sem("xr_loaded"), sem("resid")
        ln2, ln2_pow, ln2_norm = sem("ln2"), sem("ln2_pow"), sem("ln2_norm")
        stored = sem("stored")

        block = ctx.enter_context(nc.Block())
        LAST = GROUPS - 1

        def has(g):
            return not isinstance(g, int) or 0 <= g <= LAST

        def later(g):
            return not isinstance(g, int) or g > 0

        def periods(eng, period, first=-2):
            for p in range(first, 3):
                period(p)
            with eng.Fori(3, GROUPS - 2) as p:
                period(p)
            for p in range(GROUPS - 2, GROUPS + 2):
                period(p)


        @block.sync
        def _(sp):
            sp.dma_start(a_sb, a_heads.rearrange("h (w o) -> h w o", w=2).partition_broadcast(P)).then_inc(s_load_front, 16)
            for ft in range(FT):
                sp.dma_start(Wh_raw[ft], W_heads[:, ft * P:(ft + 1) * P, :].rearrange("h p o -> p h o")).then_inc(s_load_front, 16)
            for d in range(2):
                sp.dma_start(x_sb[d * N:(d + 1) * N], graphs(0)).then_inc(x_loaded, 16)
            for b in range(2):
                sp.dma_start(adj_sb[b * N:(b + 1) * N], adj).then_inc(s_adj, 16)
            sp.dma_start(ao_sb, a_out.rearrange("(w o) -> w o", w=2).partition_broadcast(P)).then_inc(s_load, 16)
            sp.dma_start(Wo_raw[:, :, 0:O], W_out.rearrange("(k p) o -> p k o", p=P)).then_inc(s_load, 16)
            sp.dma_start(b1_sb, b1.rearrange("(t p) -> p t", p=P), allow_slow_non_contiguous=True).then_inc(s_load, 16)
            for dst, src in ((b2_sb, b2), (gamma_sb, ln_gamma), (beta_sb, ln_beta)):
                sp.dma_start(dst, src.partition_broadcast(P)).then_inc(s_load, 16)

            sp.wait_ge(s_weights, 2)
            sp.wait_ge(s_front, 2)
            for i, w in enumerate((w1, w2)):
                sp.dma_start(w12_raw[:, i], w.rearrange("(k p) o -> p k o", p=P)).then_inc(s_load_w12, 16)

            def load_x(g):
                if not has(g) or (isinstance(g, int) and g == 0):
                    return
                sp.wait_ge(xs_done, g)
                sp.wait_ge(xt_done, g)
                for d in range(2):
                    sp.dma_start(x_sb[d * N:(d + 1) * N], graphs(g)).then_inc(x_loaded, 16)

            def load_xr(g):
                if not has(g):
                    return
                if later(g):
                    sp.wait_ge(stored, 16 * g)
                else:
                    sp.wait_ge(s_b2, 1)
                sp.dma_start(xr, rows(x_rows, g)).then_inc(xr_loaded, 16)

            def store(g):
                if not has(g):
                    return
                sp.wait_ge(ln2_norm, g + 1)
                sp.dma_start(rows(out_rows, g), xr).then_inc(stored, 16)

            def period(p):
                load_x(p + 2)
                store(p - 2)
                load_xr(p - 1)
            periods(sp, period)
            sp.wait_ge(stored, 16 * GROUPS)

        @block.gpsimd
        def _(pool):
            g_ = nc.gpsimd
            g_.memset(ident, 0.0).then_inc(s_const, 1)
            pool.wait_ge(s_const, 1)
            g_.affine_select(out=ident, in_=ident, compare_op=ALU.not_equal, fill=1.0, base=0,
                             pattern=[[-1, P]], channel_multiplier=1).then_inc(s_const, 1)
            pool.wait_ge(s_front, 1)

            def low_part(lo, raw, hi, n):
                pool.wait_ge(s_wcopy, n)
                g_.tensor_sub(lo, raw, hi.bitcast(F32)).then_inc(s_weights, 1)

            def split_x(g):
                if not has(g):
                    return
                pool.wait_ge(xh_done, g + 1)
                if has(g - 3):
                    pool.wait_ge(ol_done, g - 2)
                elif g > 0:
                    pool.wait_ge(diag_ready, 2 * (g + 1))
                else:
                    pool.wait_ge(s_weights, 2)
                s = slice(N, P)
                g_.tensor_sub(x_split[s], x_sb[s], x_split[s].bitcast(F32)).then_inc(xs_done, 1)
                pool.wait_ge(xs_done, g + 1)

            def spread_f2(g):
                if not has(g):
                    return
                if later(g):
                    pool.wait_ge(s_done, g)
                for i, f2 in enumerate((f2_hi.bitcast(F32), f2_lo)):
                    pool.wait_ge(f_out, 3 * g + 2 + i)
                    g_.tensor_mul(diag[:, i].rearrange("p t h m -> p (t h) m"),
                                  ident64.unsqueeze(1).broadcast_to([P, T * HD, N]),
                                  f2.rearrange("p t h -> p (t h)").unsqueeze(2).broadcast_to([P, T * HD, N])
                                  ).then_inc(diag_ready, 1)

            def spread_g2(g):
                if not has(g):
                    return
                if later(g):
                    pool.wait_ge(s2_done, g)
                for i, g2 in enumerate((g2_hi.bitcast(F32), g2_lo)):
                    pool.wait_ge(g12_out, 4 * g + 3 + i)
                    g_.tensor_mul(diag2[:, i], ident64.unsqueeze(1).broadcast_to([P, T, N]),
                                  g2.unsqueeze(2).broadcast_to([P, T, N])).then_inc(diag2_ready, 1)

            def h_low(g, h):
                if not has(g):
                    return
                if h == 0 and later(g):
                    pool.wait_ge(w_done, 2 * g)
                pool.wait_ge(h_elu, 4 * g + h + 1)
                pool.wait_ge(hh_done, 4 * g + h + 1)
                g_.tensor_sub(h_lo[:, h], h_full[h % 2], h_hi[:, h].bitcast(F32)).then_inc(hl_done, 1)

            def o_low(g):
                if not has(g):
                    return
                if later(g):
                    pool.wait_ge(ff_done, g)
                pool.wait_ge(o_elu, g + 1)
                pool.wait_ge(oh_done, g + 1)
                g_.tensor_sub(o_lo, o_full, o_hi.bitcast(F32)).then_inc(ol_done, 1)

            def inverse_root(g, ln, mv_eps, rs, done):
                if not has(g):
                    return
                pool.wait_ge(ln, 4 * g + 3)
                g_.tensor_tensor(rs, mv_eps, half, ALU.pow).then_inc(done, 1)

            def residual(g):
                if not has(g):
                    return
                pool.wait_ge(xr_loaded, 16 * (g + 1))
                g_.tensor_add(xr, xr, beta_sb.unsqueeze(1).broadcast_to([P, T, O])).then_inc(resid, 1)
                pool.wait_ge(ln1_norm, g + 1)
                g_.tensor_mul(yn, yn, gamma_sb.unsqueeze(1).broadcast_to([P, T, O])).then_inc(resid, 1)
                pool.wait_ge(resid, 3 * g + 2)
                g_.tensor_add(xr, yn, xr).then_inc(resid, 1)

            def period(p):
                for h in range(HD):
                    h_low(p, h)
                spread_f2(p + 2)
                o_low(p - 1)
                if isinstance(p, int) and p == -2:
                    low_part(w1_lo, w12_raw[:, 0], w1_hi, 3)
                    low_part(w2_lo, w12_raw[:, 1], w2_hi, 4)
                    low_part(Wo_lo, Wo_raw, Wo_hi, 5)
                else:
                    split_x(p + 2)
                residual(p - 2)
                inverse_root(p - 2, ln2, ve2, rs2, ln2_pow)
                spread_g2(p)
                inverse_root(p - 1, ln1, ve1, rs1, ln1_pow)
            for ft in range(FT):
                low_part(W_lo[:, ft], Wh_raw[ft], W_hi[:, ft], ft + 1)
            split_x(0)
            periods(pool, period)

        @block.scalar
        def _(act):
            s_ = nc.scalar

            def copy(dst, src):
                return s_.activation(dst, src, ACT.Copy)

            act.wait_ge(s_load_front, 16 * 3)
            for ft in range(FT):
                copy(W_hi[:, ft], Wh_raw[ft]).then_inc(s_wcopy, 1)

            def x_high(g):
                if not has(g):
                    return
                if later(g):
                    act.wait_ge(y_done, 4 * g)
                act.wait_ge(x_loaded, 32 * (g + 1))
                copy(x_split, x_sb).then_inc(xh_done, 1)

            def xt_copy(g):
                if not has(g):
                    return
                act.wait_ge(xt_done, g + 1)
                if later(g):
                    act.wait_ge(f_done, g)
                else:
                    act.wait_ge(s_front, 2)
                copy(xT, light[0]).then_inc(xt_out, 1)

            def exp_1(g):
                if not has(g):
                    return
                act.wait_ge(sm1, 9 * g + 6)
                s_.activation(e1, e1, ACT.Exp).then_inc(exp1, 1)

            def repeat_att(g):
                if not has(g):
                    return
                act.wait_ge(sm1, 9 * g + 9)
                a = att1.rearrange("p t h d m -> p (t h) d m")
                copy(a[:, :, 1], a[:, :, 0]).then_inc(att_twice, 1)

            def exp_2(g):
                if not has(g):
                    return
                act.wait_ge(sm2, 9 * g + 6)
                s_.activation(e2, e2, ACT.Exp).then_inc(exp2, 1)

            def pt_high(g, u):
                if not has(g):
                    return
                act.wait_ge(pt_done, 2 * g + u + 1)
                if u == 0 and later(g):
                    act.wait_ge(y_done, 4 * g)
                copy(att1T_hi[:, 2 * u:2 * u + 2].rearrange("p t h n -> p t (h n)"), light[u]).then_inc(pt_hi, 1)

            def y_high(g, t):
                if not has(g):
                    return
                act.wait_ge(y_done, 4 * g + t + 1)
                if t == 0 and later(g):
                    act.wait_ge(h_done, 4 * g)
                copy(Y_hi[:, :, :, t].rearrange("p f h n -> p (f h) n"),
                     heavy[t % 2].rearrange("p f (h n) -> p (f h) n", n=P)).then_inc(y_hi, 1)

            def h_exps(g, h):
                if not has(g):
                    return
                act.wait_ge(h_done, 4 * g + h + 1)
                if h > 1 or later(g):
                    act.wait_ge(hl_done, 4 * g + h - 1)
                s_.activation(h_full[h % 2], heavy[h % 2], ACT.Exp).then_inc(h_expd, 1)

            def h_high(g, h):
                if not has(g):
                    return
                act.wait_ge(h_elu, 4 * g + h + 1)
                if h == 0 and later(g):
                    act.wait_ge(w_done, 2 * g)
                copy(h_hi[:, h], h_full[h % 2]).then_inc(hh_done, 1)

            def w_high(g, u):
                if not has(g):
                    return
                act.wait_ge(w_done, 2 * g + u + 1)
                if u == 0 and later(g):
                    act.wait_ge(o_done, g)
                copy(wh_hi[:, 2 * u:2 * u + 2], heavy[u][:, :, 0:O]).then_inc(w_hi_s, 1)

            def pt2_high(g):
                if not has(g):
                    return
                act.wait_ge(pt2_done, g + 1)
                if later(g):
                    act.wait_ge(o_done, g)
                copy(att2T_hi.rearrange("p t n -> p (t n)"), light[1][:, 0]).then_inc(pt2_hi, 1)

            def o_exps(g):
                if not has(g):
                    return
                act.wait_ge(o_done, g + 1)
                if later(g):
                    act.wait_ge(ol_done, g)
                s_.activation(o_full, light[1], ACT.Exp).then_inc(o_expd, 1)

            def o_high(g):
                if not has(g):
                    return
                act.wait_ge(o_elu, g + 1)
                if later(g):
                    act.wait_ge(ff_done, g)
                copy(o_hi, o_full).then_inc(oh_done, 1)

            def h1_act(g):
                if not has(g):
                    return
                act.wait_ge(h1_done, g + 1)
                if later(g):
                    act.wait_ge(h1l_done, g)
                s_.activation(h1_full[:, 0], light[1][:, 0], ACT.Relu, bias=b1_sb[:, 0:1])
                s_.activation(h1_full[:, 1], light[1][:, 1], ACT.Relu, bias=b1_sb[:, 1:2]).then_inc(h1_relu, 1)
                act.wait_ge(h1_relu, g + 1)
                if later(g):
                    act.wait_ge(ff_done, g)
                copy(h1_hi, h1_full).then_inc(h1h_done, 1)

            def norm(dst, src, rs, nm, done):
                for t in range(T):
                    last = s_.activation(dst[:, t], src[:, t], ACT.Identity, bias=nm[:, t:t + 1], scale=rs[:, t:t + 1])
                last.then_inc(done, 1)

            def norm_1(g):
                if not has(g):
                    return
                act.wait_ge(ln1, 4 * g + 4)
                if later(g):
                    act.wait_ge(resid, 3 * g)
                norm(yn, tiles(light[1], O), rs1, nm1, ln1_norm)

            def norm_2(g):
                if not has(g):
                    return
                act.wait_ge(ln2, 4 * g + 4)
                norm(xr, xr, rs2, nm2, ln2_norm)

            x_high(0)

            def period(p):
                h_exps(p, 0)
                norm_1(p - 2)
                h_high(p, 0)
                h_exps(p, 1)
                exp_2(p - 1)
                h_exps(p, 2)
                h_high(p, 1)
                pt_high(p + 1, 0)
                pt_high(p + 1, 1)
                h_high(p, 2)
                h_exps(p, 3)
                xt_copy(p + 2)
                pt2_high(p - 1)
                y_high(p + 1, 0)
                h_high(p, 3)
                y_high(p + 1, 1)
                o_exps(p - 1)
                y_high(p + 1, 2)
                o_high(p - 1)
                y_high(p + 1, 3)
                if isinstance(p, int) and p == -2:
                    act.wait_ge(s_load_w12, 16 * 2)
                    copy(w1_hi, w12_raw[:, 0]).then_inc(s_wcopy, 1)
                    copy(w2_hi, w12_raw[:, 1]).then_inc(s_wcopy, 1)
                    act.wait_ge(s_wo, 1)
                    copy(Wo_hi, Wo_raw).then_inc(s_wcopy, 1)
                else:
                    x_high(p + 2)
                w_high(p, 0)
                exp_1(p + 2)
                h1_act(p - 1)
                repeat_att(p + 2)
                w_high(p, 1)
                norm_2(p - 2)
            periods(act, period)

        @block.vector
        def _(dve):
            v_ = nc.vector
            setup = [0]

            def link(ins):
                setup[0] += 1
                ins.then_inc(s_setup, 1)
                dve.wait_ge(s_setup, setup[0])

            v_.memset(half, -0.5)
            v_.memset(ones_b, 1.0)
            v_.memset(att2, 0.0)
            v_.memset(b2_rows, 0.0)
            ones = block_ones.bitcast(F32)
            link(v_.memset(ones, 0.0))
            v_.memset(ones[0:N, 0:N], 1.0)
            v_.memset(ones[N:P, N:P], 1.0)
            dve.wait_ge(s_const, 2)
            v_.tensor_copy(ident_r, ident)
            v_.tensor_copy(ident_b, ident)
            v_.tensor_add(ident64, ident[:, 0:N], ident[:, N:P]).then_inc(s_front, 1)
            dve.wait_ge(s_load_front, 16 * 3)
            for ft in range(FT):
                for h in range(HD):
                    for w in range(2):
                        last = v_.tensor_tensor_reduce(out=product[2 * h + w], in0=Wh_raw[ft][:, h], in1=a_sb[:, h, w],
                                                       scale=1.0, scalar=0.0, op0=ALU.mult, op1=ALU.add,
                                                       accum_out=score_w[:, ft, w, h:h + 1])
                if ft == 0:
                    link(last)
            last.then_inc(s_front, 1)

            def mask():
                dve.wait_ge(s_adj, 16 * 2)
                link(v_.tensor_scalar(mask64, adj_sb, 0.0, BIG, ALU.is_gt, ALU.mult))
                v_.tensor_scalar(mask_b.rearrange("p u h m -> p (u h) m"), mask64.unsqueeze(1).broadcast_to([P, 2 * HD, N]),
                                 -BIG, None, ALU.add).then_inc(s_front, 1)

            def score_columns():
                dve.wait_ge(s_load, 16 * 6)
                for w in range(2):
                    for k in range(KT):
                        last = v_.tensor_tensor_reduce(out=product[k], in0=Wo_raw[:, k, 0:O], in1=ao_sb[:, w], scale=1.0,
                                                       scalar=0.0, op0=ALU.mult, op1=ALU.add,
                                                       accum_out=Wo_raw[:, k, O + w:O + w + 1])
                    if w == 0:
                        link(last)
                last.then_inc(s_wo, 1)

            def b2_parts():
                for i in range(3):
                    link(v_.tensor_copy(b2_p, b2_r if i else b2_sb))
                    last = v_.tensor_copy(b2_rows[32 * i:32 * i + 1], b2_p[32 * i:32 * i + 1])
                    if i < 2:
                        link(v_.tensor_sub(b2_r, b2_r if i else b2_sb, b2_p))
                last.then_inc(s_b2, 1)

            def f_copy(g):
                if not has(g):
                    return
                dve.wait_ge(f_done, g + 1)
                if later(g):
                    dve.wait_ge(diag_ready, 2 * g)
                v_.tensor_copy(f12, light[0][:, 0, 0:T * 2 * HD].rearrange("p (t w h) -> p w t h", w=2, h=HD)
                               ).then_inc(f_out, 1)
                dve.wait_ge(f_out, 3 * g + 1)
                v_.tensor_copy(f2_hi, f12[:, 1]).then_inc(f_out, 1)
                dve.wait_ge(f_out, 3 * g + 2)
                v_.tensor_sub(f2_lo, f12[:, 1], f2_hi.bitcast(F32)).then_inc(f_out, 1)

            def scores(g, done, sm, psum, own, e, mx, ml, read):
                dve.wait_ge(done, g + 1)
                if later(g):
                    dve.wait_ge(read, g)
                J = e.shape[1]
                own_b = own.unsqueeze(2).broadcast_to([P, J, N])
                v_.reduce_max(mx, psum, axis=X).then_inc(sm, 1)
                v_.tensor_add(e, psum, own_b).then_inc(sm, 1)
                dve.wait_ge(sm, 9 * g + 1)
                v_.tensor_add(mx, mx, own).then_inc(sm, 1)
                dve.wait_ge(sm, 9 * g + 2)
                v_.scalar_tensor_tensor(e, e, ALPHA, e, ALU.mult, ALU.max).then_inc(sm, 1)
                dve.wait_ge(sm, 9 * g + 3)
                v_.scalar_tensor_tensor(ml, mx, ALPHA, mx, ALU.mult, ALU.max).then_inc(sm, 1)
                dve.wait_ge(sm, 9 * g + 5)
                v_.tensor_sub(e, e, ml.unsqueeze(2).broadcast_to([P, J, N])).then_inc(sm, 1)

            def softmax(g, exp, sm, e, z, att, transposed, n):
                dve.wait_ge(exp, g + 1)
                J = e.shape[1]
                v_.reduce_sum(z, e, axis=X).then_inc(sm, 1)
                dve.wait_ge(sm, 9 * g + 7)
                v_.reciprocal(z, z).then_inc(sm, 1)
                dve.wait_ge(sm, 9 * g + 8)
                if later(g):
                    dve.wait_ge(transposed, n * g)
                halves = [(slice(0, P), slice(0, N))] if att.shape[2] == N else \
                    [(slice(b * N, (b + 1) * N),) * 2 for b in range(2)]
                for s, c in halves:
                    last = v_.tensor_mul(att[s, :, c], e[s], z[s].unsqueeze(2).broadcast_to([s.stop - s.start, J, N]))
                last.then_inc(sm, 1)

            def flat(ap):
                return ap.rearrange("p t h m -> p (t h) m")

            def row(ap):
                return ap.rearrange("p t h -> p (t h)")

            def scores_1(g):
                if has(g):
                    scores(g, s_done, sm1, tiles(light[0], HD * N).rearrange("p t (h m) -> p (t h) m", m=N),
                           row(f12[:, 0]), flat(e1), row(mx1), row(ml1), exp1)

            def softmax_1(g):
                if has(g):
                    softmax(g, exp1, sm1, flat(e1), row(z1), att1.rearrange("p t h d m -> p (t h) d m")[:, :, 0], pt_done, 2)

            def scores_2(g):
                if has(g):
                    scores(g, s2_done, sm2, light[0][:, 0, 0:T * N].rearrange("p (t m) -> p t m", m=N),
                           g12[:, :, 0:1].rearrange("p t c -> p (t c)"), e2, mx2, ml2, exp2)

            def softmax_2(g):
                if has(g):
                    softmax(g, exp2, sm2, e2, z2, att2, pt2_done, 1)

            def pt_low(g, u):
                if not has(g):
                    return
                dve.wait_ge(pt_hi, 2 * g + u + 1)
                if u == 0 and later(g):
                    dve.wait_ge(y_done, 4 * g)
                hi, lo = ((a[:, 2 * u:2 * u + 2].rearrange("p t h n -> p t (h n)")) for a in (att1T_hi, att1T_lo))
                v_.tensor_sub(lo, light[u], hi.bitcast(F32)).then_inc(pt_lo, 1)

            def y_low(g, t):
                if not has(g):
                    return
                dve.wait_ge(y_hi, 4 * g + t + 1)
                if t == 0 and later(g):
                    dve.wait_ge(h_done, 4 * g)
                hi, lo = (a[:, :, :, t].rearrange("p f h n -> p (f h) n") for a in (Y_hi, Y_lo))
                v_.tensor_sub(lo, heavy[t % 2].rearrange("p f (h n) -> p (f h) n", n=P), hi.bitcast(F32)
                              ).then_inc(y_lo, 1)

            def h_finish(g, h):
                if not has(g):
                    return
                dve.wait_ge(h_expd, 4 * g + h + 1)
                full = h_full[h % 2]
                v_.tensor_scalar(full, full, 1.0, -1.0, ALU.min, ALU.add).then_inc(h_min, 1)
                dve.wait_ge(h_min, 4 * g + h + 1)
                v_.tensor_max(full, heavy[h % 2], full).then_inc(h_elu, 1)

            def w_low(g, u):
                if not has(g):
                    return
                dve.wait_ge(w_hi_s, 2 * g + u + 1)
                if u == 0 and later(g):
                    dve.wait_ge(o_done, g)
                t = slice(2 * u, 2 * u + 2)
                v_.tensor_sub(wh_lo[:, t], heavy[u][:, :, 0:O], wh_hi[:, t].bitcast(F32)).then_inc(w_lo_s, 1)
                v_.tensor_copy(g12[:, t], heavy[u][:, :, O:WC]).then_inc(g12_out, 1)
                if u == 1:
                    g2 = g12[:, :, 1:2].rearrange("p t c -> p (t c)")
                    if later(g):
                        dve.wait_ge(diag2_ready, 2 * g)
                    dve.wait_ge(g12_out, 4 * g + 2)
                    v_.tensor_copy(g2_hi, g2).then_inc(g12_out, 1)
                    dve.wait_ge(g12_out, 4 * g + 3)
                    v_.tensor_sub(g2_lo, g2, g2_hi.bitcast(F32)).then_inc(g12_out, 1)

            def pt2_low(g):
                if not has(g):
                    return
                dve.wait_ge(pt2_hi, g + 1)
                if later(g):
                    dve.wait_ge(o_done, g)
                v_.tensor_sub(att2T_lo.rearrange("p t n -> p (t n)"), light[1][:, 0],
                              att2T_hi.rearrange("p t n -> p (t n)").bitcast(F32)).then_inc(pt2_lo, 1)

            def o_finish(g):
                if not has(g):
                    return
                dve.wait_ge(o_expd, g + 1)
                v_.tensor_scalar(o_full, o_full, 1.0, -1.0, ALU.min, ALU.add).then_inc(o_min, 1)
                dve.wait_ge(o_min, g + 1)
                v_.tensor_max(o_full, light[1], o_full).then_inc(o_elu, 1)

            def h1_low(g):
                if not has(g):
                    return
                dve.wait_ge(h1h_done, g + 1)
                if later(g):
                    dve.wait_ge(ff_done, g)
                v_.tensor_sub(h1_lo, h1_full, h1_hi.bitcast(F32)).then_inc(h1l_done, 1)

            def stats(g, ln, src, st, mv, ve):
                for t in range(T):
                    last = v_.bn_stats(st[:, t], src[:, t])
                last.then_inc(ln, 1)
                dve.wait_ge(ln, 4 * g + 1)
                v_.memset(spare, 0.0)
                for t in range(T):
                    last = v_.bn_aggr(mv[:, t], st[:, t])
                last.then_inc(ln, 1)
                dve.wait_ge(ln, 4 * g + 2)
                v_.tensor_scalar(ve.unsqueeze(2), mv[:, :, 1:2], EPS, None, ALU.add).then_inc(ln, 1)

            def shift(g, ln, pw, mv, rs, nm):
                dve.wait_ge(pw, g + 1)
                v_.scalar_tensor_tensor(nm.unsqueeze(2), mv[:, :, 0:1], -1.0, rs.unsqueeze(2), ALU.mult, ALU.mult
                                        ).then_inc(ln, 1)

            def stats_1(g):
                if has(g):
                    dve.wait_ge(ff_done, g + 1)
                    if later(g):
                        dve.wait_ge(ln1_norm, g)
                    stats(g, ln1, tiles(light[1], O), st1, mv1, ve1)

            def shift_1(g):
                if has(g):
                    shift(g, ln1, ln1_pow, mv1, rs1, nm1)

            def stats_2(g):
                if has(g):
                    dve.wait_ge(resid, 3 * g + 3)
                    if later(g):
                        dve.wait_ge(ln2_norm, g)
                    stats(g, ln2, xr, st2, mv2, ve2)

            def shift_2(g):
                if has(g):
                    shift(g, ln2, ln2_pow, mv2, rs2, nm2)

            def period(p):
                shift_1(p - 2)
                h_finish(p, 0)
                scores_2(p - 1)
                h_finish(p, 1)
                softmax_2(p - 1)
                h_finish(p, 2)
                pt_low(p + 1, 0)
                pt_low(p + 1, 1)
                h_finish(p, 3)
                pt2_low(p - 1)
                y_low(p + 1, 0)
                y_low(p + 1, 1)
                f_copy(p + 2)
                o_finish(p - 1)
                y_low(p + 1, 2)
                y_low(p + 1, 3)
                scores_1(p + 2)
                w_low(p, 0)
                softmax_1(p + 2)
                h1_low(p - 1)
                stats_2(p - 2)
                w_low(p, 1)
                shift_2(p - 2)
                stats_1(p - 1)
            mask()
            f_copy(0)
            score_columns()
            scores_1(0)
            b2_parts()
            softmax_1(0)
            periods(dve, period, first=-1)

        @block.tensor
        def _(pe):
            mm = nc.tensor.matmul

            def three(out_, pairs, first=True, last=True):
                n = len(pairs)
                for i, ((ahi, alo), (bhi, blo)) in enumerate(pairs):
                    mm(out_, ahi, bhi, start=first and i == 0, stop=False)
                    mm(out_, ahi, blo, start=False, stop=False)
                    ins = mm(out_, alo, bhi, start=False, stop=last and i == n - 1)
                return ins

            pe.wait_ge(s_front, 1)

            def x_transpose(g):
                if not has(g):
                    return
                pe.wait_ge(x_loaded, 32 * (g + 1))
                if has(g - 1):
                    pe.wait_ge(pt_lo, 2 * (g - 1) + 1)
                mm(light[0][:, 0, 0:2], ident_b, ident_b[:, 0:2], start=True, stop=True)
                for b in range(2 * T):
                    for ft in range(FT):
                        ins = nc.tensor.transpose(light[0][:, ft, b * N:(b + 1) * N], x_sb[0:N, b, ft * P:(ft + 1) * P],
                                                  ident[0:N, 0:N])
                ins.then_inc(xt_done, 1)

            def score_terms(g):
                if not has(g):
                    return
                pe.wait_ge(xt_out, g + 1)
                if not later(g):
                    pe.wait_ge(s_front, 2)
                for t in range(T):
                    for ft in range(FT):
                        ins = mm(light[0][:, 0, t * 2 * HD:(t + 1) * 2 * HD], xT[:, ft, t * P:(t + 1) * P],
                                 score_w[:, ft].rearrange("p w h -> p (w h)"), start=ft == 0, stop=ft == FT - 1)
                ins.then_inc(f_done, 1)

            def score_spread(g):
                if not has(g):
                    return
                if not later(g):
                    pe.wait_ge(s_front, 3)
                pe.wait_ge(diag_ready, 2 * (g + 1))
                for u in range(2):
                    mm(light[0][:, u], ident_b, mask_b.rearrange("p u h m -> p (u h m)"), start=True, stop=False)
                    for i in range(2):
                        ins = mm(light[0][:, u], block_ones, diag[:, i, 2 * u:2 * u + 2].rearrange("p t h m -> p (t h m)"),
                                 start=False, stop=i == 1)
                ins.then_inc(s_done, 1)

            def att_transpose(g, u):
                if not has(g):
                    return
                if u == 0:
                    pe.wait_ge(att_twice, g + 1)
                    if has(g - 2):
                        pe.wait_ge(sm2, 9 * (g - 2) + 2)
                elif has(g - 3):
                    pe.wait_ge(ln1_norm, g - 2)
                for t in range(2 * u, 2 * u + 2):
                    for h in range(HD):
                        twice = att1[:, t, h].rearrange("p d m -> p (d m)")
                        ins = nc.tensor.transpose(light[u][:, t - 2 * u, h * P:(h + 1) * P], twice, ident)
                ins.then_inc(pt_done, 1)

            def attend(g, t):
                if not has(g):
                    return
                pe.wait_ge(xs_done, g + 1)
                pe.wait_ge(pt_lo, 2 * g + t // 2 + 1)
                if t < 2:
                    if has(g - 1):
                        pe.wait_ge(h_elu, 4 * (g - 1) + 3 + t)
                else:
                    pe.wait_ge(y_lo, 4 * g + t - 1)
                for ft in range(FT):
                    for b in range(2):
                        n = slice(b * N, (b + 1) * N)
                        ps = heavy[t % 2][:, ft].rearrange("p (h n) -> p h n", n=P)[:, :, n]
                        xs = x_split[:, 2 * t + b, ft * P:(ft + 1) * P]
                        mm(ps, xs, att1T_hi[:, t, :, n], start=True, stop=False)
                        ins = mm(ps, xs, att1T_lo[:, t, :, n], start=False, stop=True)
                ins.then_inc(y_done, 1)

            def head(g, h):
                if not has(g):
                    return
                if h == 0:
                    pe.wait_ge(y_lo, 4 * g + 4)
                if h < 2:
                    if has(g - 1):
                        pe.wait_ge(g12_out, 4 * (g - 1) + h + 1)
                else:
                    pe.wait_ge(h_elu, 4 * g + h - 1)
                for ot in range(OT):
                    o = slice(ot * P, (ot + 1) * P)
                    ins = three(heavy[h % 2][:, ot],
                                [((W_hi[:, ft, h, o], W_lo[:, ft, h, o]),
                                  (Y_hi[:, ft, h].rearrange("p t n -> p (t n)"), Y_lo[:, ft, h].rearrange("p t n -> p (t n)")))
                                 for ft in range(FT)])
                ins.then_inc(h_done, 1)

            def project(g, u):
                if not has(g):
                    return
                if u == 0:
                    pe.wait_ge(hl_done, 4 * g + 4)
                if has(g + 1):
                    pe.wait_ge(y_lo, 4 * (g + 1) + 3 + u)
                else:
                    pe.wait_ge(h_elu, 4 * g + 3 + u)
                for t in range(2 * u, 2 * u + 2):
                    n = slice(t * P, (t + 1) * P)
                    ins = three(heavy[u][:, t - 2 * u, 0:WC],
                                [((h_hi[:, k // OT, k % OT, n], h_lo[:, k // OT, k % OT, n]), (Wo_hi[:, k], Wo_lo[:, k]))
                                 for k in range(KT)])
                ins.then_inc(w_done, 1)

            def score_spread_2(g):
                if not has(g):
                    return
                pe.wait_ge(diag2_ready, 2 * (g + 1))
                if has(g + 2):
                    pe.wait_ge(sm1, 9 * (g + 2) + 2)
                ps = light[0][:, 0, 0:T * N]
                mm(ps, ident_b, mask_b[:, 0].rearrange("p h m -> p (h m)"), start=True, stop=False)
                for i in range(2):
                    ins = mm(ps, block_ones, diag2[:, i].rearrange("p t m -> p (t m)"), start=False, stop=i == 1)
                ins.then_inc(s2_done, 1)

            def att2_transpose(g):
                if not has(g):
                    return
                pe.wait_ge(sm2, 9 * g + 9)
                if has(g + 2):
                    pe.wait_ge(pt_lo, 2 * (g + 2) + 2)
                elif later(g):
                    pe.wait_ge(ln1_norm, g)
                for t in range(T):
                    ins = nc.tensor.transpose(light[1][:, 0, t * P:(t + 1) * P], att2[:, t], ident)
                ins.then_inc(pt2_done, 1)

            def attend_2(g):
                if not has(g):
                    return
                pe.wait_ge(pt2_lo, g + 1)
                pe.wait_ge(w_lo_s, 2 * g + 2)
                for t in range(T):
                    n = slice(t * P, (t + 1) * P)
                    for ot in range(OT):
                        o = slice(ot * P, (ot + 1) * P)
                        ins = three(light[1][:, ot, n], [((wh_hi[:, t, o], wh_lo[:, t, o]), (att2T_hi[:, t], att2T_lo[:, t]))])
                ins.then_inc(o_done, 1)

            def ffn_in(g):
                if not has(g):
                    return
                pe.wait_ge(ol_done, g + 1)
                for ft in range(OT):
                    f = slice(ft * P, (ft + 1) * P)
                    ins = three(light[1][:, ft], [((w1_hi[:, ot, f], w1_lo[:, ot, f]), (o_hi[:, ot], o_lo[:, ot]))
                                                  for ot in range(OT)])
                ins.then_inc(h1_done, 1)

            def ffn_out(g):
                if not has(g):
                    return
                pe.wait_ge(h1l_done, g + 1)
                ps = tiles(light[1], O)
                for t in range(T):
                    n = slice(t * P, (t + 1) * P)
                    mm(ps[:, t], ones_b, b2_rows, start=True, stop=False)
                    three(ps[:, t], [((h1_hi[:, ft, n], h1_lo[:, ft, n]), (w2_hi[:, ft], w2_lo[:, ft])) for ft in range(OT)],
                          first=False, last=False)
                    for ot in range(OT):
                        o = slice(ot * P, (ot + 1) * P)
                        mm(ps[:, t, o], o_hi[:, ot, n], ident_r, start=False, stop=False)
                        ins = mm(ps[:, t, o], o_lo[:, ot, n], ident_r, start=False, stop=ot == OT - 1)
                ins.then_inc(ff_done, 1)

            def period(p):
                if isinstance(p, int) and p == 0:
                    pe.wait_ge(s_weights, 5)
                if isinstance(p, int) and p == 1:
                    pe.wait_ge(s_b2, 1)
                head(p, 0)
                score_spread_2(p - 1)
                head(p, 1)
                head(p, 2)
                att_transpose(p + 1, 0)
                att_transpose(p + 1, 1)
                head(p, 3)
                x_transpose(p + 2)
                att2_transpose(p - 1)
                attend(p + 1, 0)
                attend(p + 1, 1)
                score_terms(p + 2)
                attend_2(p - 1)
                attend(p + 1, 2)
                attend(p + 1, 3)
                score_spread(p + 2)
                project(p, 0)
                ffn_in(p - 1)
                project(p, 1)
                ffn_out(p - 1)
            periods(pe, period)


INPUTS = ["x", "adj", "L0_gnn_W_heads", "L0_gnn_a_heads", "L0_gnn_W_out", "L0_gnn_a_out", "L0_gnn_w1", "L0_gnn_b1",
          "L0_gnn_w2", "L0_gnn_b2", "L0_gnn_ln_gamma", "L0_gnn_ln_beta"]


def kernel(**inputs):
    import numpy as _np
    import concourse.bacc as _bacc
    from concourse import mybir as _mybir
    from concourse.bass_utils import run_bass_kernel_spmd as _run

    nc = _bacc.Bacc("TRN2", target_bir_lowering=False, num_devices=1)
    arrays, args = {}, []
    for name in INPUTS:
        a = _np.ascontiguousarray(inputs[name])
        arrays[f"in_{name}"] = a
        args.append(nc.dram_tensor(f"in_{name}", a.shape, _mybir.dt.from_np(a.dtype), kind="ExternalInput").ap())
    shape = inputs["x"].shape
    args.append(nc.dram_tensor("out_0", shape, _mybir.dt.float32, kind="ExternalOutput").ap())
    build(nc, *args)
    return _run(nc, [arrays], core_ids=[0]).results[0]["out_0"]
```

```python
from contextlib import ExitStack

import numpy as np
import concourse.bass as bass
from concourse import mybir

F32 = mybir.dt.float32
F32R = mybir.dt.float32r
BF16 = mybir.dt.bfloat16
I32 = mybir.dt.int32
ALU = mybir.AluOpType
ACT = mybir.ActivationFunctionType
X = mybir.AxisListType.X

P = 128
T = 4
BIG = float(2.0 ** 100)
ALPHA = 0.01
EPS = 1e-5


def build(nc, x, adj, W_heads, a_heads, W_out, a_out, w1, b1, w2, b2, ln_gamma, ln_beta, out):
    B, N, F = x.shape
    HD, _, O = W_heads.shape
    FT, OT = F // P, O // P
    KT = HD * OT
    GROUPS = B * N // (P * T)
    ROWS = P * T
    WC = O + 2
    assert N * 2 == P and F == O == 256 and HD == 4

    x_rows = x.rearrange("b n f -> (b n) f")
    out_rows = out.rearrange("b n f -> (b n) f")

    def graphs(g):
        return x[bass.ds(g * 2 * T, 2 * T)].rearrange("b m f -> m b f")

    def rows(ap, g):
        return ap[bass.ds(g * ROWS, ROWS), :].rearrange("(t p) f -> p t f", p=P)

    with ExitStack() as ctx:
        def sb(name, shape, dt=F32):
            return ctx.enter_context(nc.sbuf_tensor(name, [P] + shape, dt))[:]

        def sem(name):
            return ctx.enter_context(nc.semaphore(name))

        ident = sb("ident", [P])
        ident_b = sb("ident_b", [P], BF16)
        ident64 = sb("ident64", [N])
        block_ones = sb("block_ones", [P], F32R)
        ones_b = sb("ones_b", [P], BF16)
        adj_sb = sb("adj_sb", [N], I32)
        mask64 = sb("mask64", [N])
        mask_b = sb("mask_b", [2, HD, N], BF16)
        half = sb("half", [T])
        W_hi, W_lo = sb("W_hi", [FT, HD, O], F32R), sb("W_lo", [FT, HD, O], F32R)
        Wo_hi, Wo_lo = sb("Wo_hi", [KT, WC], F32R), sb("Wo_lo", [KT, WC], F32R)
        w1_hi, w1_lo = sb("w1_hi", [OT, O], F32R), sb("w1_lo", [OT, O], F32R)
        w2_hi, w2_lo = sb("w2_hi", [OT, O], F32R), sb("w2_lo", [OT, O], F32R)
        score_w = sb("score_w", [FT, 2, HD])
        b1_sb = sb("b1_sb", [OT])
        b2_rows = sb("b2_rows", [O], BF16)
        gamma_sb, beta_sb = sb("gamma_sb", [O]), sb("beta_sb", [O])

        x_sb = sb("x_sb", [2 * T, F])
        x_hi, x_lo = sb("x_hi", [2 * T, F], F32R), sb("x_lo", [2 * T, F], F32R)
        f12 = sb("f12", [2, T, HD])
        f2_hi, f2_lo = sb("f2_hi", [T, HD], F32R), sb("f2_lo", [T, HD])
        diag = sb("diag", [2, T, HD, N], F32R)
        score_work = sb("score_work", [3, T * HD * N])
        e1 = score_work[:, 0].rearrange("p (t h m) -> p t h m", t=T, h=HD)
        att1 = score_work[:, 1:3].rearrange("p i k -> p (i k)").rearrange("p (t h d m) -> p t h d m", t=T, h=HD, d=2)
        xT = score_work[:, 0].rearrange("p (f n) -> p f n", f=FT)
        mx1, ml1, z1 = sb("mx1", [T, HD]), sb("ml1", [T, HD]), sb("z1", [T, HD])
        att1T = sb("att1T", [T, HD, P], F32R)
        Y_hi, Y_lo = sb("Y_hi", [FT, HD, T, P], F32R), sb("Y_lo", [FT, HD, T, P], F32R)
        h_work = sb("h_work", [max(2 * OT * ROWS, KT * WC)])
        h_full = [h_work[:, i * OT * ROWS:(i + 1) * OT * ROWS].rearrange("p (o n) -> p o n", o=OT) for i in range(2)]
        h_hi, h_lo = sb("h_hi", [HD, OT, ROWS], F32R), sb("h_lo", [HD, OT, ROWS], F32R)
        wh_hi, wh_lo = sb("wh_hi", [T, O], F32R), sb("wh_lo", [T, O], F32R)
        g12 = sb("g12", [T, 2])
        g2_hi, g2_lo = sb("g2_hi", [T], F32R), sb("g2_lo", [T])
        diag2 = diag.rearrange("p i t h m -> p (i t h m)")[:, 0:2 * T * N].rearrange("p (i t m) -> p i t m", i=2, t=T)
        e2 = score_work[:, 0, 0:T * N].rearrange("p (t m) -> p t m", m=N)
        mx2, ml2, z2 = sb("mx2", [T]), sb("ml2", [T]), sb("z2", [T])
        att2 = sb("att2", [T, P])
        att2T_hi, att2T_lo = sb("att2T_hi", [T, P], F32R), sb("att2T_lo", [T, P], F32R)
        o_full = sb("o_full", [T, O])
        o_hi, o_lo = sb("o_hi", [OT, ROWS], F32R), sb("o_lo", [OT, ROWS], F32R)
        h1_full = sb("h1_full", [OT, ROWS])
        z_full = h1_full.rearrange("p o n -> p (o n)").rearrange("p (t o) -> p t o", o=O)
        spare = sb("spare", [1])
        st1, mv1 = sb("st1", [T, 6]), sb("mv1", [T, 2])
        rs1, nm1, ve1 = sb("rs1", [T]), sb("nm1", [T]), sb("ve1", [T])
        st2, mv2 = sb("st2", [T, 6]), sb("mv2", [T, 2])
        rs2, nm2, ve2 = sb("rs2", [T]), sb("nm2", [T]), sb("ve2", [T])
        xr = sb("xr", [T, F])

        xT_1 = h1_full

        xr_last, o_full_last = x_sb[:, 0:T], x_sb[:, T:2 * T]
        o_parts_last, h1_parts_last = ([v[:, i * T:(i + 1) * T].rearrange("p t f -> p (t f)").rearrange("p (o n) -> p o n", o=OT)
                                        for v in (x_hi, x_lo)] for i in range(2))

        a_sb = score_work[:, 1:3].rearrange("p i (h w o) -> p (i h) w o", w=2, o=O)
        Wh_raw = [o_full, h1_full.rearrange("p o n -> p (o n)").rearrange("p (h o) -> p h o", h=HD)]
        Wo_raw = h_work[:, 0:KT * WC].rearrange("p (k c) -> p k c", c=WC)
        w12_raw = o_full.rearrange("p (i k) o -> p i k o", i=2)
        ao_sb, b2_sb, b2_r = xr[:, 0:2], xr[:, 2], xr[:, 3]
        b2_p = sb("b2_p", [O], BF16)

        heavy = [ctx.enter_context(nc.psum_tensor(f"heavy{i}", [P, 2, 512], F32))[:] for i in range(2)]
        light = [ctx.enter_context(nc.psum_tensor(f"light{i}", [P, 2, 512], F32))[:] for i in range(2)]

        product = [heavy[i // 4].rearrange("p b (c o) -> p (b c) o", o=O)[:, i % 4] for i in range(8)]

        def tiles(ap, c):
            return ap.rearrange("p b (u c) -> p (b u) c", c=c)

        s_load_a, s_load = sem("s_load_a"), sem("s_load")
        s_load_w = [sem(f"s_load_w{ft}") for ft in range(FT)]
        s_load_w12 = sem("s_load_w12")
        s_adj = sem("s_adj")
        s_const = sem("s_const")
        s_setup = sem("s_setup")
        s_front = sem("s_front")
        s_wo = sem("s_wo")
        s_wcopy = sem("s_wcopy")
        s_weights = sem("s_weights")
        s_b2 = sem("s_b2")
        x_loaded = [sem("x_upper"), sem("x_lower")]
        xh_done, xs_done = sem("xh_done"), sem("xs_done")
        xt_done, xt_out = sem("xt_done"), sem("xt_out")
        f_done, f_out = sem("f_done"), sem("f_out")
        diag_ready = sem("diag_ready")
        s_done, sm1, exp1 = sem("s_done"), sem("sm1"), sem("exp1")
        ah_done, al_done = sem("ah_done"), sem("al_done")
        pt_done, pt_out = sem("pt_done"), sem("pt_out")
        y_done, y_hi, y_lo = sem("y_done"), sem("y_hi"), sem("y_lo")
        h_done, h_expd, h_elu = sem("h_done"), sem("h_expd"), sem("h_elu")
        h_min = sem("h_min")
        hh_done, hl_done = sem("hh_done"), sem("hl_done")
        w_done, w_hi_s, w_lo_s = sem("w_done"), sem("w_hi_s"), sem("w_lo_s")
        g12_out, diag2_ready = sem("g12_out"), sem("diag2_ready")
        s2_done, sm2, exp2 = sem("s2_done"), sem("sm2"), sem("exp2")
        pt2_done, pt2_hi, pt2_lo = sem("pt2_done"), sem("pt2_hi"), sem("pt2_lo")
        o_done, o_expd = sem("o_done"), sem("o_expd")
        o_min, o_elu = sem("o_min"), sem("o_elu")
        ot_done = sem("ot_done")
        oh_done, ol_done = sem("oh_done"), sem("ol_done")
        h1_done, h1_relu = sem("h1_done"), sem("h1_relu")
        h1h_done, h1l_done = sem("h1h_done"), sem("h1l_done")
        ff_done, ff_sum = sem("ff_done"), sem("ff_sum")
        ln1, ln1_pow, ln1_norm = sem("ln1"), sem("ln1_pow"), sem("ln1_norm")
        xr_loaded, resid = sem("xr_loaded"), sem("resid")
        xr_beta, scaled = sem("xr_beta"), sem("scaled")
        ln2, ln2_pow, ln2_norm = sem("ln2"), sem("ln2_pow"), sem("ln2_norm")
        stored = sem("stored")
        xr_last_loaded, stored_last = sem("xr_last_loaded"), sem("stored_last")
        ln2_norm_a, ln2_norm_b = sem("ln2_norm_a"), sem("ln2_norm_b")
        xr_last_beta = sem("xr_last_beta")

        block = ctx.enter_context(nc.Block())
        LAST = GROUPS - 1

        def has(g):
            return not isinstance(g, int) or 0 <= g <= LAST

        def later(g):
            return not isinstance(g, int) or g > 0

        def is_last(g):
            return isinstance(g, int) and g == LAST

        def back(g):
            return heavy[1] if is_last(g) else light[1]

        def o_place(g):
            return o_full_last if is_last(g) else o_full

        def h1_place(g):
            return o_full.rearrange("p t o -> p (t o)").rearrange("p (o n) -> p o n", o=OT) if is_last(g) else h1_full

        def z_place(g):
            return o_full_last if is_last(g) else z_full

        def o_parts(g):
            return o_parts_last if is_last(g) else (o_hi, o_lo)

        def h1_parts(g):
            return h1_parts_last if is_last(g) else (o_hi, o_lo)

        def parts(g):
            return [(1, slice(0, 1)), (2, slice(1, 2))] if is_last(g) else [(1, slice(0, 2))]

        def residual_place(g):
            return xr_last if is_last(g) else xr

        def pt_place(g, u):
            return heavy[1] if isinstance(g, int) and g == 0 and u == 0 else light[u]

        def pt_half(copy, g, u):
            return copy(att1T[:, 2 * u:2 * u + 2].rearrange("p t h n -> p t (h n)"), pt_place(g, u))

        def times_gamma(eng, place):
            return eng.tensor_mul(place, place, gamma_sb.unsqueeze(1).broadcast_to([P, T, O]))

        def plus_beta(eng, place):
            return eng.tensor_add(place, place, beta_sb.unsqueeze(1).broadcast_to([P, T, O]))

        def spread(eng, i, f2):
            return eng.tensor_mul(diag[:, i].rearrange("p t h m -> p (t h) m"), ident64.unsqueeze(1).broadcast_to([P, T * HD, N]),
                                  f2.rearrange("p t h -> p (t h)").unsqueeze(2).broadcast_to([P, T * HD, N]))

        def att_low_part(eng):
            a = att1.rearrange("p t h d m -> p (t h) d m")
            return eng.tensor_sub(a[:, :, 1].bitcast(F32R), e1.rearrange("p t h m -> p (t h) m"), a[:, :, 0])

        def periods(eng, period):
            for p in range(3):
                period(p)
            with eng.Fori(3, GROUPS - 2) as p:
                period(p)
            period(GROUPS - 2)

        @block.sync
        def _(sp):
            sp.dma_start(a_sb, a_heads.rearrange("h (w o) -> h w o", w=2).partition_broadcast(P)).then_inc(s_load_a, 16)
            for ft in range(FT):
                sp.dma_start(Wh_raw[ft], W_heads[:, ft * P:(ft + 1) * P, :].rearrange("h p o -> p h o")).then_inc(s_load_w[ft], 16)
                sp.dma_start(x_sb[ft * N:(ft + 1) * N], graphs(0)).then_inc(x_loaded[ft], 16)
            for b in range(2):
                sp.dma_start(adj_sb[b * N:(b + 1) * N], adj).then_inc(s_adj, 16)
            sp.dma_start(ao_sb, a_out.rearrange("(w o) -> w o", w=2).partition_broadcast(P)).then_inc(s_load, 16)
            sp.dma_start(Wo_raw[:, :, 0:O], W_out.rearrange("(k p) o -> p k o", p=P)).then_inc(s_load, 16)
            sp.dma_start(b1_sb, b1.rearrange("(t p) -> p t", p=P), allow_slow_non_contiguous=True).then_inc(s_load, 16)
            for dst, src in ((b2_sb, b2), (gamma_sb, ln_gamma), (beta_sb, ln_beta)):
                sp.dma_start(dst, src.partition_broadcast(P)).then_inc(s_load, 16)

            sp.wait_ge(s_weights, 2)
            sp.wait_ge(s_front, 2)
            for i, w in enumerate((w1, w2)):
                sp.dma_start(w12_raw[:, i], w.rearrange("(k p) o -> p k o", p=P)).then_inc(s_load_w12, 16)

            def load_x(g):
                if not has(g):
                    return
                sp.wait_ge(xs_done, g)
                sp.wait_ge(xt_done, g)
                for d in range(2):
                    sp.dma_start(x_sb[d * N:(d + 1) * N], graphs(g)).then_inc(x_loaded[d], 16)

            def load_xr(g):
                if not has(g):
                    return
                if is_last(g):
                    sp.wait_ge(xs_done, g + 1)
                    sp.wait_ge(xt_done, g + 1)
                    sp.dma_start(xr_last, rows(x_rows, g)).then_inc(xr_last_loaded, 16)
                    return
                if later(g):
                    sp.wait_ge(stored, 16 * g)
                else:
                    sp.wait_ge(s_b2, 1)
                sp.dma_start(xr, rows(x_rows, g)).then_inc(xr_loaded, 16)

            def store(g):
                if not has(g):
                    return
                if is_last(g):
                    for n, (a, b) in zip((ln2_norm_a, ln2_norm_b), ((0, T // 2), (T // 2, T))):
                        sp.wait_ge(n, 1)
                        sp.dma_start(rows(out_rows, g)[:, a:b], xr_last[:, a:b]).then_inc(stored_last, 16)
                    return
                sp.wait_ge(ln2_norm, g + 1)
                sp.dma_start(rows(out_rows, g), xr).then_inc(stored, 16)

            def period(p):
                load_x(p + 2)
                store(p - 2)
                load_xr(p - 1)
            load_x(1)
            periods(sp, period)
            load_xr(LAST)
            period(LAST)
            store(LAST - 1)
            store(LAST)
            sp.wait_ge(stored, 16 * LAST)
            sp.wait_ge(stored_last, 16 * 2)

        @block.gpsimd
        def _(pool):
            g_ = nc.gpsimd
            g_.memset(ident, 0.0).then_inc(s_const, 1)
            pool.wait_ge(s_const, 1)
            g_.affine_select(out=ident, in_=ident, compare_op=ALU.not_equal, fill=1.0, base=0,
                             pattern=[[-1, P]], channel_multiplier=1).then_inc(s_const, 1)
            pool.wait_ge(s_front, 1)

            def low_part(lo, raw, hi, n):
                pool.wait_ge(s_wcopy, n)
                g_.tensor_sub(lo, raw, hi.bitcast(F32)).then_inc(s_weights, 1)

            def split_x(g):
                if not has(g):
                    return
                pool.wait_ge(xh_done, g + 1)
                g_.tensor_sub(x_lo, x_sb, x_hi.bitcast(F32)).then_inc(xs_done, 1)

            def att_low(g):
                if not has(g):
                    return
                pool.wait_ge(ah_done, g + 1)
                att_low_part(g_).then_inc(al_done, 1)

            def spread_f2_high(g):
                if not has(g):
                    return
                if later(g):
                    pool.wait_ge(s_done, g)
                pool.wait_ge(f_out, 3 * g + 2)
                spread(g_, 0, f2_hi.bitcast(F32)).then_inc(diag_ready, 1)

            def spread_g2(g):
                if not has(g):
                    return
                if later(g):
                    pool.wait_ge(s2_done, g)
                for i, g2 in enumerate((g2_hi.bitcast(F32), g2_lo)):
                    pool.wait_ge(g12_out, 4 * g + 3 + i)
                    g_.tensor_mul(diag2[:, i], ident64.unsqueeze(1).broadcast_to([P, T, N]),
                                  g2.unsqueeze(2).broadcast_to([P, T, N])).then_inc(diag2_ready, 1)

            def h_low(g, h):
                if not has(g):
                    return
                if h == 0 and later(g):
                    pool.wait_ge(w_done, 2 * g)
                pool.wait_ge(h_elu, 4 * g + h + 1)
                pool.wait_ge(hh_done, 4 * g + h + 1)
                g_.tensor_sub(h_lo[:, h], h_full[h % 2], h_hi[:, h].bitcast(F32)).then_inc(hl_done, 1)

            def inverse_root(g, ln, mv_eps, rs, done):
                if not has(g):
                    return
                pool.wait_ge(ln, 4 * g + 3)
                g_.tensor_tensor(rs, mv_eps, half, ALU.pow).then_inc(done, 1)

            def add_beta(g):
                if has(g):
                    pool.wait_ge(xr_loaded, 16 * (g + 1))
                    plus_beta(g_, xr).then_inc(xr_beta, 1)

            def scale(g):
                if has(g):
                    pool.wait_ge(ln1_norm, g + 1)
                    times_gamma(g_, z_full).then_inc(scaled, 1)

            def add_residual(g):
                if has(g):
                    pool.wait_ge(xr_beta, g + 1)
                    pool.wait_ge(scaled, g + 1)
                    g_.tensor_add(xr, z_full, xr).then_inc(resid, 1)

            def period(p):
                h_low(p, 0)
                h_low(p, 1)
                h_low(p, 2)
                spread_f2_high(p + 2)
                h_low(p, 3)
                add_beta(p - 2)
                scale(p - 2)
                add_residual(p - 2)
                split_x(p + 2)
                att_low(p + 2)
                inverse_root(p - 2, ln2, ve2, rs2, ln2_pow)
                spread_g2(p)
                inverse_root(p - 1, ln1, ve1, rs1, ln1_pow)

            for ft in range(FT):
                low_part(W_lo[:, ft], Wh_raw[ft], W_hi[:, ft], ft + 1)
            spread_f2_high(0)
            low_part(w1_lo, w12_raw[:, 0], w1_hi, 3)
            low_part(w2_lo, w12_raw[:, 1], w2_hi, 4)
            spread_f2_high(1)
            low_part(Wo_lo, Wo_raw, Wo_hi, 5)
            split_x(1)
            periods(pool, period)

            g = LAST
            h_low(g, 0)
            h_low(g, 1)
            h_low(g, 2)
            add_beta(g - 2)
            scale(g - 2)
            add_residual(g - 2)
            inverse_root(g - 2, ln2, ve2, rs2, ln2_pow)
            spread_g2(g)
            inverse_root(g - 1, ln1, ve1, rs1, ln1_pow)
            add_beta(g - 1)
            inverse_root(g - 1, ln2, ve2, rs2, ln2_pow)
            inverse_root(g, ln1, ve1, rs1, ln1_pow)
            inverse_root(g, ln2, ve2, rs2, ln2_pow)

        @block.scalar
        def _(act):
            s_ = nc.scalar

            def copy(dst, src):
                return s_.activation(dst, src, ACT.Copy)

            for ft in range(FT):
                act.wait_ge(s_load_w[ft], 16)
                copy(W_hi[:, ft], Wh_raw[ft]).then_inc(s_wcopy, 1)

            def x_high(g):
                if not has(g):
                    return
                if later(g):
                    act.wait_ge(y_done, 4 * g)
                for d in range(2):
                    act.wait_ge(x_loaded[d], 16 * (g + 1))
                copy(x_hi, x_sb).then_inc(xh_done, 1)

            def xt_copy(g):
                if not has(g):
                    return
                act.wait_ge(xt_done, g + 1)
                if isinstance(g, int) and g == 1:
                    act.wait_ge(s_weights, 2)
                    act.wait_ge(s_front, 2)
                    copy(xT_1, light[0]).then_inc(xt_out, 1)
                    return
                if later(g):
                    act.wait_ge(al_done, g)
                if has(g - 3):
                    act.wait_ge(sm2, 9 * (g - 3) + 9)
                copy(xT, light[0]).then_inc(xt_out, 1)

            def exp_1(g):
                if not has(g):
                    return
                act.wait_ge(sm1, 9 * g + 6)
                s_.activation(e1, e1, ACT.Exp).then_inc(exp1, 1)

            def att_high(g):
                if not has(g):
                    return
                act.wait_ge(sm1, 9 * g + 9)
                copy(att1.rearrange("p t h d m -> p (t h) d m")[:, :, 0].bitcast(F32R), e1.rearrange("p t h m -> p (t h) m")
                     ).then_inc(ah_done, 1)

            def exp_2(g):
                if not has(g):
                    return
                act.wait_ge(sm2, 9 * g + 6)
                s_.activation(e2, e2, ACT.Exp).then_inc(exp2, 1)

            def pt_copy(g, u):
                if not has(g):
                    return
                act.wait_ge(pt_done, 2 * g + 2 - u)
                if later(g):
                    act.wait_ge(y_done, 4 * g)
                pt_half(copy, g, u).then_inc(pt_out, 1)

            def y_high(g, t):
                if not has(g):
                    return
                act.wait_ge(y_done, 4 * g + t + 1)
                if t == 0 and later(g):
                    act.wait_ge(h_done, 4 * g)
                copy(Y_hi[:, :, :, t].rearrange("p f h n -> p (f h) n"),
                     heavy[t % 2].rearrange("p f (h n) -> p (f h) n", n=P)).then_inc(y_hi, 1)

            def h_exps(g, h):
                if not has(g):
                    return
                act.wait_ge(h_done, 4 * g + h + 1)
                if h > 1 or later(g):
                    act.wait_ge(hl_done, 4 * g + h - 1)
                s_.activation(h_full[h % 2], heavy[h % 2], ACT.Exp).then_inc(h_expd, 1)

            def h_high(g, h):
                if not has(g):
                    return
                act.wait_ge(h_elu, 4 * g + h + 1)
                if h == 0 and later(g):
                    act.wait_ge(w_done, 2 * g)
                copy(h_hi[:, h], h_full[h % 2]).then_inc(hh_done, 1)

            def w_high(g, u):
                if not has(g):
                    return
                act.wait_ge(w_done, 2 * g + u + 1)
                if u == 0 and later(g):
                    act.wait_ge(o_done, g)
                copy(wh_hi[:, 2 * u:2 * u + 2], heavy[u][:, :, 0:O]).then_inc(w_hi_s, 1)

            def pt2_high(g):
                if not has(g):
                    return
                act.wait_ge(pt2_done, g + 1)
                if later(g):
                    act.wait_ge(o_done, g)
                copy(att2T_hi.rearrange("p t n -> p (t n)"), back(g)[:, 0]).then_inc(pt2_hi, 1)

            def o_exps(g):
                if not has(g):
                    return
                act.wait_ge(o_done, g + 1)
                if later(g) and not is_last(g):
                    act.wait_ge(ff_sum, g)
                s_.activation(o_place(g), tiles(back(g), O), ACT.Exp).then_inc(o_expd, 1)

            def o_high(g):
                if not has(g):
                    return
                if later(g) and not is_last(g):
                    act.wait_ge(ff_done, g)
                for i, o in parts(g):
                    act.wait_ge(ot_done, g + i)
                    copy(o_parts(g)[0][:, o], back(g)[:, o]).then_inc(oh_done, 1)

            def h1_act(g):
                if not has(g):
                    return
                if is_last(g):
                    act.wait_ge(ff_sum, g)
                elif later(g):
                    act.wait_ge(resid, g)
                h1 = h1_place(g)
                for i, f in parts(g):
                    act.wait_ge(h1_done, g + i)
                    for ft in range(f.start, f.stop):
                        last = s_.activation(h1[:, ft], back(g)[:, ft], ACT.Relu, bias=b1_sb[:, ft:ft + 1])
                    last.then_inc(h1_relu, 1)
                    act.wait_ge(h1_relu, g + i)
                    copy(h1_parts(g)[0][:, f], h1[:, f]).then_inc(h1h_done, 1)

            def norm(dst, src, rs, nm, done):
                for t in range(T):
                    last = s_.activation(dst[:, t], src[:, t], ACT.Identity, bias=nm[:, t:t + 1], scale=rs[:, t:t + 1])
                last.then_inc(done, 1)

            def norm_1(g):
                if not has(g):
                    return
                act.wait_ge(ln1, 4 * g + 4)
                norm(z_full, z_full, rs1, nm1, ln1_norm)

            def norm_2(g):
                if not has(g):
                    return
                act.wait_ge(ln2, 4 * g + 4)
                norm(xr, xr, rs2, nm2, ln2_norm)

            def period(p):
                h_exps(p, 0)
                if isinstance(p, int) and p == 0:
                    exp_1(1)
                h_exps(p, 1)
                h_high(p, 0)
                exp_2(p - 1)
                if isinstance(p, int) and p == 0:
                    att_high(1)
                else:
                    pt_copy(p + 1, 1)
                h_high(p, 1)
                h_exps(p, 2)
                if isinstance(p, int) and p == 0:
                    pt_copy(1, 1)
                pt_copy(p + 1, 0)
                h_exps(p, 3)
                xt_copy(p + 2)
                h_high(p, 2)
                pt2_high(p - 1)
                y_high(p + 1, 0)
                y_high(p + 1, 1)
                h_high(p, 3)
                y_high(p + 1, 2)
                o_exps(p - 1)
                y_high(p + 1, 3)
                norm_1(p - 2)
                o_high(p - 1)
                x_high(p + 2)
                w_high(p, 0)
                exp_1(p + 2)
                h1_act(p - 1)
                att_high(p + 2)
                w_high(p, 1)
                norm_2(p - 2)

            xt_copy(0)
            x_high(0)
            act.wait_ge(s_load_w12, 16 * 2)
            copy(w1_hi, w12_raw[:, 0]).then_inc(s_wcopy, 1)
            copy(w2_hi, w12_raw[:, 1]).then_inc(s_wcopy, 1)
            exp_1(0)
            xt_copy(1)
            att_high(0)
            pt_copy(0, 1)
            y_high(0, 0)
            y_high(0, 1)
            act.wait_ge(s_wo, 2)
            copy(Wo_hi, Wo_raw).then_inc(s_wcopy, 1)
            y_high(0, 2)
            y_high(0, 3)
            x_high(1)
            periods(act, period)

            g = LAST
            h_exps(g, 0)
            h_exps(g, 1)
            h_high(g, 0)
            exp_2(g - 1)
            h_high(g, 1)
            h_exps(g, 2)
            pt2_high(g - 1)
            h_exps(g, 3)
            h_high(g, 2)
            h_high(g, 3)
            o_exps(g - 1)
            norm_1(g - 2)
            o_high(g - 1)
            w_high(g, 0)
            w_high(g, 1)
            h1_act(g - 1)
            exp_2(g)
            norm_2(g - 2)
            pt2_high(g)
            o_exps(g)
            o_high(g)
            h1_act(g)
            norm_2(g - 1)
            act.wait_ge(ln2, 4 * g + 4)
            for t in range(T // 2):
                last = s_.activation(xr_last[:, t], xr_last[:, t], ACT.Identity, bias=nm2[:, t:t + 1], scale=rs2[:, t:t + 1])
            last.then_inc(ln2_norm_a, 1)

        @block.vector
        def _(dve):
            v_ = nc.vector
            setup = [0]

            def link(ins):
                setup[0] += 1
                ins.then_inc(s_setup, 1)
                dve.wait_ge(s_setup, setup[0])

            v_.memset(half, -0.5)
            v_.memset(ones_b, 1.0)
            v_.memset(att2, 0.0)
            v_.memset(b2_rows, 0.0)
            ones = block_ones.bitcast(F32)
            link(v_.memset(ones, 0.0))
            v_.memset(ones[0:N, 0:N], 1.0)
            v_.memset(ones[N:P, N:P], 1.0)
            dve.wait_ge(s_const, 2)
            v_.tensor_copy(ident_b, ident)
            v_.tensor_add(ident64, ident[:, 0:N], ident[:, N:P]).then_inc(s_front, 1)
            dve.wait_ge(s_load_a, 16)
            for ft in range(FT):
                dve.wait_ge(s_load_w[ft], 16)
                for h in range(HD):
                    for w in range(2):
                        last = v_.tensor_tensor_reduce(out=product[2 * h + w], in0=Wh_raw[ft][:, h], in1=a_sb[:, h, w],
                                                       scale=1.0, scalar=0.0, op0=ALU.mult, op1=ALU.add,
                                                       accum_out=score_w[:, ft, w, h:h + 1])
                if ft == 0:
                    link(last)
            last.then_inc(s_front, 1)

            def mask():
                dve.wait_ge(s_adj, 16 * 2)
                link(v_.tensor_scalar(mask64, adj_sb, 0.0, BIG, ALU.is_gt, ALU.mult))
                v_.tensor_scalar(mask_b.rearrange("p u h m -> p (u h) m"), mask64.unsqueeze(1).broadcast_to([P, 2 * HD, N]),
                                 -BIG, None, ALU.add).then_inc(s_front, 1)

            def score_column(w):
                dve.wait_ge(s_load, 16 * 6)
                dve.wait_ge(s_weights, 4)
                for k in range(KT):
                    last = v_.tensor_tensor_reduce(out=o_full[:, k % 4], in0=Wo_raw[:, k, 0:O], in1=ao_sb[:, w], scale=1.0,
                                                   scalar=0.0, op0=ALU.mult, op1=ALU.add,
                                                   accum_out=Wo_raw[:, k, O + w:O + w + 1])
                    if k % 4 == 3 and k < KT - 1:
                        link(last)
                last.then_inc(s_wo, 1)
                if w == 0:
                    dve.wait_ge(s_wo, 1)

            def b2_parts():
                for i in range(3):
                    link(v_.tensor_copy(b2_p, b2_r if i else b2_sb))
                    last = v_.tensor_copy(b2_rows[32 * i:32 * i + 1], b2_p[32 * i:32 * i + 1])
                    if i < 2:
                        link(v_.tensor_sub(b2_r, b2_r if i else b2_sb, b2_p))
                last.then_inc(s_b2, 1)

            def f_copy(g):
                if not has(g):
                    return
                dve.wait_ge(f_done, g + 1)
                if later(g):
                    dve.wait_ge(diag_ready, 2 * g)
                v_.tensor_copy(f12, light[0][:, 0, 0:T * 2 * HD].rearrange("p (t w h) -> p w t h", w=2, h=HD)
                               ).then_inc(f_out, 1)
                dve.wait_ge(f_out, 3 * g + 1)
                v_.tensor_copy(f2_hi, f12[:, 1]).then_inc(f_out, 1)
                dve.wait_ge(f_out, 3 * g + 2)
                v_.tensor_sub(f2_lo, f12[:, 1], f2_hi.bitcast(F32)).then_inc(f_out, 1)

            def att_low_early(g):
                dve.wait_ge(ah_done, g + 1)
                att_low_part(v_).then_inc(al_done, 1)

            def spread_f2_low(g):
                if not has(g):
                    return
                if later(g):
                    dve.wait_ge(s_done, g)
                dve.wait_ge(f_out, 3 * g + 3)
                spread(v_, 1, f2_lo).then_inc(diag_ready, 1)

            def score_max(g, done, sm, psum, mx):
                dve.wait_ge(done, g + 1)
                v_.reduce_max(mx, psum, axis=X).then_inc(sm, 1)

            def score_sums(g, sm, psum, own, e, mx, read):
                if later(g):
                    dve.wait_ge(read, g)
                v_.tensor_add(e, psum, own.unsqueeze(2).broadcast_to([P, e.shape[1], N])).then_inc(sm, 1)
                dve.wait_ge(sm, 9 * g + 1)
                v_.tensor_add(mx, mx, own).then_inc(sm, 1)

            def score_relu(g, sm, e, mx, ml):
                dve.wait_ge(sm, 9 * g + 2)
                v_.scalar_tensor_tensor(e, e, ALPHA, e, ALU.mult, ALU.max).then_inc(sm, 1)
                dve.wait_ge(sm, 9 * g + 3)
                v_.scalar_tensor_tensor(ml, mx, ALPHA, mx, ALU.mult, ALU.max).then_inc(sm, 1)
                dve.wait_ge(sm, 9 * g + 5)
                v_.tensor_sub(e, e, ml.unsqueeze(2).broadcast_to([P, e.shape[1], N])).then_inc(sm, 1)

            def softmax(g, exp, sm, e, z, att, transposed, n):
                dve.wait_ge(exp, g + 1)
                J = e.shape[1]
                v_.reduce_sum(z, e, axis=X).then_inc(sm, 1)
                dve.wait_ge(sm, 9 * g + 7)
                v_.reciprocal(z, z).then_inc(sm, 1)
                dve.wait_ge(sm, 9 * g + 8)
                if later(g):
                    dve.wait_ge(transposed, n * g)
                halves = [(slice(0, P), slice(0, N))] if att.shape[2] == N else \
                    [(slice(b * N, (b + 1) * N),) * 2 for b in range(2)]
                for s, c in halves:
                    last = v_.tensor_mul(att[s, :, c], e[s], z[s].unsqueeze(2).broadcast_to([s.stop - s.start, J, N]))
                last.then_inc(sm, 1)

            def flat(ap):
                return ap.rearrange("p t h m -> p (t h) m")

            def row(ap):
                return ap.rearrange("p t h -> p (t h)")

            scores_psum_1 = tiles(light[0], HD * N).rearrange("p t (h m) -> p (t h) m", m=N)
            scores_psum_2 = light[0][:, 0, 0:T * N].rearrange("p (t m) -> p t m", m=N)

            def score_max_1(g):
                if has(g):
                    score_max(g, s_done, sm1, scores_psum_1, row(mx1))

            def score_sums_1(g):
                if has(g):
                    score_sums(g, sm1, scores_psum_1, row(f12[:, 0]), flat(e1), row(mx1), al_done)

            def score_relu_1(g):
                if has(g):
                    score_relu(g, sm1, flat(e1), row(mx1), row(ml1))

            def scores_1(g):
                score_max_1(g)
                score_sums_1(g)
                score_relu_1(g)

            def softmax_1(g):
                if has(g):
                    softmax(g, exp1, sm1, flat(e1), row(z1), flat(e1), pt_done, 2)

            def scores_2(g):
                if has(g):
                    score_max(g, s2_done, sm2, scores_psum_2, mx2)
                    score_sums(g, sm2, scores_psum_2, g12[:, :, 0:1].rearrange("p t c -> p (t c)"), e2, mx2, exp2)
                    score_relu(g, sm2, e2, mx2, ml2)

            def softmax_2(g):
                if has(g):
                    softmax(g, exp2, sm2, e2, z2, att2, pt2_done, 1)

            def y_low(g, t):
                if not has(g):
                    return
                dve.wait_ge(y_hi, 4 * g + t + 1)
                if t == 0 and later(g):
                    dve.wait_ge(h_done, 4 * g)
                hi, lo = (a[:, :, :, t].rearrange("p f h n -> p (f h) n") for a in (Y_hi, Y_lo))
                v_.tensor_sub(lo, heavy[t % 2].rearrange("p f (h n) -> p (f h) n", n=P), hi.bitcast(F32)
                              ).then_inc(y_lo, 1)

            def h_finish(g, h):
                if not has(g):
                    return
                dve.wait_ge(h_expd, 4 * g + h + 1)
                full = h_full[h % 2]
                v_.tensor_scalar(full, full, 1.0, -1.0, ALU.min, ALU.add).then_inc(h_min, 1)
                dve.wait_ge(h_min, 4 * g + h + 1)
                v_.tensor_max(full, heavy[h % 2], full).then_inc(h_elu, 1)

            def w_low(g, u):
                if not has(g):
                    return
                dve.wait_ge(w_hi_s, 2 * g + u + 1)
                if u == 0 and later(g):
                    dve.wait_ge(o_done, g)
                t = slice(2 * u, 2 * u + 2)
                v_.tensor_sub(wh_lo[:, t], heavy[u][:, :, 0:O], wh_hi[:, t].bitcast(F32)).then_inc(w_lo_s, 1)
                v_.tensor_copy(g12[:, t], heavy[u][:, :, O:WC]).then_inc(g12_out, 1)
                if u == 1:
                    g2 = g12[:, :, 1:2].rearrange("p t c -> p (t c)")
                    if later(g):
                        dve.wait_ge(diag2_ready, 2 * g)
                    dve.wait_ge(g12_out, 4 * g + 2)
                    v_.tensor_copy(g2_hi, g2).then_inc(g12_out, 1)
                    dve.wait_ge(g12_out, 4 * g + 3)
                    v_.tensor_sub(g2_lo, g2, g2_hi.bitcast(F32)).then_inc(g12_out, 1)

            def pt2_low(g):
                if not has(g):
                    return
                dve.wait_ge(pt2_hi, g + 1)
                if later(g):
                    dve.wait_ge(o_done, g)
                v_.tensor_sub(att2T_lo.rearrange("p t n -> p (t n)"), back(g)[:, 0],
                              att2T_hi.rearrange("p t n -> p (t n)").bitcast(F32)).then_inc(pt2_lo, 1)

            def o_min1(g):
                if has(g):
                    dve.wait_ge(o_expd, g + 1)
                    v_.tensor_scalar(o_place(g), o_place(g), 1.0, -1.0, ALU.min, ALU.add).then_inc(o_min, 1)

            def o_max(g):
                if has(g):
                    dve.wait_ge(o_min, g + 1)
                    v_.tensor_max(o_place(g), tiles(back(g), O), o_place(g)).then_inc(o_elu, 1)

            def o_low(g):
                if has(g):
                    hi, lo = o_parts(g)
                    for i, o in parts(g):
                        dve.wait_ge(oh_done, g + i)
                        v_.tensor_sub(lo[:, o], back(g)[:, o], hi[:, o].bitcast(F32)).then_inc(ol_done, 1)

            def add_out(g):
                if has(g):
                    dve.wait_ge(ff_done, g + 1)
                    v_.tensor_add(z_place(g), tiles(back(g), O), o_place(g)).then_inc(ff_sum, 1)

            def h1_low(g):
                if not has(g):
                    return
                hi, lo = h1_parts(g)
                for i, f in parts(g):
                    dve.wait_ge(h1h_done, g + i)
                    v_.tensor_sub(lo[:, f], h1_place(g)[:, f], hi[:, f].bitcast(F32)).then_inc(h1l_done, 1)

            def stats(g, ln, src, st, mv, ve):
                for t in range(T):
                    last = v_.bn_stats(st[:, t], src[:, t])
                last.then_inc(ln, 1)
                stats_end(g, ln, st, mv, ve)

            def stats_end(g, ln, st, mv, ve):
                dve.wait_ge(ln, 4 * g + 1)
                v_.memset(spare, 0.0)
                for t in range(T):
                    last = v_.bn_aggr(mv[:, t], st[:, t])
                last.then_inc(ln, 1)
                dve.wait_ge(ln, 4 * g + 2)
                v_.tensor_scalar(ve.unsqueeze(2), mv[:, :, 1:2], EPS, None, ALU.add).then_inc(ln, 1)

            def add_out_stats_last():
                g, z = LAST, z_place(LAST)
                for i, u in parts(g):
                    t = slice(2 * u.start, 2 * u.stop)
                    dve.wait_ge(ff_done, g + i)
                    v_.tensor_add(z[:, t], tiles(back(g), O)[:, t], z[:, t]).then_inc(ff_sum, 1)
                    dve.wait_ge(ff_sum, g + i)
                    for k in range(t.start, t.stop):
                        last = v_.bn_stats(st1[:, k], z[:, k])
                last.then_inc(ln1, 1)
                stats_end(g, ln1, st1, mv1, ve1)

            def shift(g, ln, pw, mv, rs, nm):
                dve.wait_ge(pw, g + 1)
                v_.scalar_tensor_tensor(nm.unsqueeze(2), mv[:, :, 0:1], -1.0, rs.unsqueeze(2), ALU.mult, ALU.mult
                                        ).then_inc(ln, 1)

            def stats_1(g):
                if has(g):
                    dve.wait_ge(ff_sum, g + 1)
                    if later(g):
                        dve.wait_ge(ln1_norm, g)
                    stats(g, ln1, z_place(g), st1, mv1, ve1)

            def shift_1(g):
                if has(g):
                    shift(g, ln1, ln1_pow, mv1, rs1, nm1)

            def gamma_fused(g):
                z = z_place(g)
                for t in range(T):
                    last = v_.scalar_tensor_tensor(z[:, t], z[:, t], mv1[:, t, 0:1], gamma_sb, ALU.subtract, ALU.mult)
                last.then_inc(ln1, 1)

            def residual_fused(g):
                z, to = z_place(g), residual_place(g)
                dve.wait_ge(ln1, 4 * g + 4)
                dve.wait_ge(ln1_pow, g + 1)
                for t in range(T):
                    last = v_.scalar_tensor_tensor(to[:, t], z[:, t], rs1[:, t:t + 1], to[:, t], ALU.mult, ALU.add)
                last.then_inc(resid, 1)

            def stats_2(g):
                if has(g):
                    dve.wait_ge(resid, g + 1)
                    if later(g):
                        dve.wait_ge(ln2_norm, g)
                    stats(g, ln2, residual_place(g), st2, mv2, ve2)

            def shift_2(g):
                if has(g):
                    shift(g, ln2, ln2_pow, mv2, rs2, nm2)

            def period(p):
                h_finish(p, 0)
                shift_1(p - 2)
                if isinstance(p, int) and p == 0:
                    softmax_1(1)
                scores_2(p - 1)
                h_finish(p, 1)
                if isinstance(p, int) and p == 0:
                    att_low_early(1)
                softmax_2(p - 1)
                h_finish(p, 2)
                h_finish(p, 3)
                pt2_low(p - 1)
                f_copy(p + 2)
                y_low(p + 1, 0)
                y_low(p + 1, 1)
                spread_f2_low(p + 2)
                y_low(p + 1, 2)
                o_min1(p - 1)
                o_max(p - 1)
                y_low(p + 1, 3)
                score_max_1(p + 2)
                o_low(p - 1)
                score_sums_1(p + 2)
                score_relu_1(p + 2)
                if isinstance(p, int) and p == 0:
                    b2_parts()
                w_low(p, 0)
                softmax_1(p + 2)
                h1_low(p - 1)
                stats_2(p - 2)
                w_low(p, 1)
                shift_2(p - 2)
                add_out(p - 1)
                stats_1(p - 1)

            mask()
            f_copy(0)
            spread_f2_low(0)
            dve.wait_ge(xh_done, 1)
            v_.tensor_sub(x_lo, x_sb, x_hi.bitcast(F32)).then_inc(xs_done, 1)
            scores_1(0)
            softmax_1(0)
            att_low_early(0)
            score_column(0)
            f_copy(1)
            dve.wait_ge(pt_done, 2)
            pt_half(v_.tensor_copy, 0, 0).then_inc(pt_out, 1)
            score_column(1)
            y_low(0, 0)
            y_low(0, 1)
            spread_f2_low(1)
            y_low(0, 2)
            y_low(0, 3)
            scores_1(1)
            periods(dve, period)

            g = LAST
            h_finish(g, 0)
            shift_1(g - 2)
            scores_2(g - 1)
            h_finish(g, 1)
            softmax_2(g - 1)
            h_finish(g, 2)
            pt2_low(g - 1)
            h_finish(g, 3)
            dve.wait_ge(hh_done, 4 * g + 4)
            dve.wait_ge(hl_done, 4 * g + 3)
            v_.tensor_sub(h_lo[:, 3], h_full[1], h_hi[:, 3].bitcast(F32)).then_inc(hl_done, 1)
            o_min1(g - 1)
            o_max(g - 1)
            o_low(g - 1)
            w_low(g, 0)
            stats_2(g - 2)
            w_low(g, 1)
            shift_2(g - 2)
            scores_2(g)
            softmax_2(g)
            h1_low(g - 1)
            pt2_low(g)
            dve.wait_ge(xr_last_loaded, 16)
            plus_beta(v_, xr_last).then_inc(xr_last_beta, 1)
            o_min1(g)
            o_max(g)
            o_low(g)
            add_out(g - 1)
            stats_1(g - 1)
            h1_low(g)
            gamma_fused(g - 1)
            dve.wait_ge(xr_beta, g)
            residual_fused(g - 1)
            stats_2(g - 1)
            add_out_stats_last()
            shift_2(g - 1)
            gamma_fused(g)
            dve.wait_ge(xr_last_beta, 1)
            residual_fused(g)
            stats_2(g)
            shift_2(g)
            dve.wait_ge(ln2, 4 * g + 4)
            for t in range(T // 2, T):
                last = v_.tensor_scalar(xr_last[:, t], xr_last[:, t], rs2[:, t:t + 1], nm2[:, t:t + 1], ALU.mult, ALU.add)
            last.then_inc(ln2_norm_b, 1)

        @block.tensor
        def _(pe):
            mm = nc.tensor.matmul

            def three(out_, pairs, first=True, last=True):
                n = len(pairs)
                for i, ((ahi, alo), (bhi, blo)) in enumerate(pairs):
                    mm(out_, ahi, bhi, start=first and i == 0, stop=False)
                    mm(out_, ahi, blo, start=False, stop=False)
                    ins = mm(out_, alo, bhi, start=False, stop=last and i == n - 1)
                return ins

            pe.wait_ge(s_front, 1)

            def x_transpose(g):
                if not has(g):
                    return
                pe.wait_ge(x_loaded[0], 16 * (g + 1))
                if isinstance(g, int) and g == 1:
                    pe.wait_ge(sm1, 2)
                elif has(g - 1):
                    pe.wait_ge(pt_out, 2 * g)
                mm(light[0][:, 0, 0:2], ident_b, ident_b[:, 0:2], start=True, stop=True)
                for b in range(2 * T):
                    for ft in range(FT):
                        ins = nc.tensor.transpose(light[0][:, ft, b * N:(b + 1) * N], x_sb[0:N, b, ft * P:(ft + 1) * P],
                                                  ident[0:N, 0:N])
                ins.then_inc(xt_done, 1)

            def score_terms(g):
                if not has(g):
                    return
                pe.wait_ge(xt_out, g + 1)
                if not later(g):
                    pe.wait_ge(s_front, 2)
                xt = xT_1 if isinstance(g, int) and g == 1 else xT
                for t in range(T):
                    for ft in range(FT):
                        ins = mm(light[0][:, 0, t * 2 * HD:(t + 1) * 2 * HD], xt[:, ft, t * P:(t + 1) * P],
                                 score_w[:, ft].rearrange("p w h -> p (w h)"), start=ft == 0, stop=ft == FT - 1)
                ins.then_inc(f_done, 1)

            def score_spread(g):
                if not has(g):
                    return
                if not later(g):
                    pe.wait_ge(s_front, 3)
                pe.wait_ge(diag_ready, 2 * (g + 1))
                for u in range(2):
                    mm(light[0][:, u], ident_b, mask_b.rearrange("p u h m -> p (u h m)"), start=True, stop=False)
                    for i in range(2):
                        ins = mm(light[0][:, u], block_ones, diag[:, i, 2 * u:2 * u + 2].rearrange("p t h m -> p (t h m)"),
                                 start=False, stop=i == 1)
                ins.then_inc(s_done, 1)

            def att_transpose(g, u):
                if not has(g):
                    return
                if u == 1:
                    pe.wait_ge(al_done, g + 1)
                    if has(g - 3):
                        pe.wait_ge(ff_sum, g - 2)
                elif has(g - 2):
                    pe.wait_ge(sm2, 9 * (g - 2) + 2)
                for t in range(2 * u, 2 * u + 2):
                    for h in range(HD):
                        ins = nc.tensor.transpose(pt_place(g, u)[:, t - 2 * u, h * P:(h + 1) * P],
                                                  att1[:, t, h].rearrange("p d m -> p (d m)"), ident)
                ins.then_inc(pt_done, 1)

            def attend(g, t):
                if not has(g):
                    return
                pe.wait_ge(xs_done, g + 1)
                pe.wait_ge(pt_out, 2 * g + 2)
                if t < 2:
                    if has(g - 1):
                        pe.wait_ge(h_elu, 4 * (g - 1) + 3 + t)
                else:
                    pe.wait_ge(y_lo, 4 * g + t - 1)
                for ft in range(FT):
                    for b in range(2):
                        n = slice(b * N, (b + 1) * N)
                        ps = heavy[t % 2][:, ft].rearrange("p (h n) -> p h n", n=P)[:, :, n]
                        for i, xs in enumerate((x_hi, x_lo)):
                            ins = mm(ps, xs[:, 2 * t + b, ft * P:(ft + 1) * P], att1T[:, t, :, n], start=i == 0, stop=i == 1)
                ins.then_inc(y_done, 1)

            def head(g, h):
                if not has(g):
                    return
                if h == 0:
                    pe.wait_ge(y_lo, 4 * g + 4)
                if h < 2:
                    if has(g - 1):
                        pe.wait_ge(g12_out, 4 * (g - 1) + h + 1)
                else:
                    pe.wait_ge(h_elu, 4 * g + h - 1)
                for ot in range(OT):
                    o = slice(ot * P, (ot + 1) * P)
                    ins = three(heavy[h % 2][:, ot],
                                [((W_hi[:, ft, h, o], W_lo[:, ft, h, o]),
                                  (Y_hi[:, ft, h].rearrange("p t n -> p (t n)"), Y_lo[:, ft, h].rearrange("p t n -> p (t n)")))
                                 for ft in range(FT)])
                ins.then_inc(h_done, 1)

            def project(g, u):
                if not has(g):
                    return
                if u == 0:
                    pe.wait_ge(hl_done, 4 * g + 3)
                if has(g + 1):
                    pe.wait_ge(y_lo, 4 * (g + 1) + 3 + u)
                else:
                    pe.wait_ge(h_elu, 4 * g + 3 + u)
                for t in range(2 * u, 2 * u + 2):
                    n = slice(t * P, (t + 1) * P)
                    for h in range(HD):
                        if t == 0 and h == HD - 1:
                            out_transpose(g - 1)
                            pe.wait_ge(hl_done, 4 * g + 4)
                        ins = three(heavy[u][:, t - 2 * u, 0:WC],
                                    [((h_hi[:, h, ot, n], h_lo[:, h, ot, n]), (Wo_hi[:, h * OT + ot], Wo_lo[:, h * OT + ot]))
                                     for ot in range(OT)], first=h == 0, last=h == HD - 1)
                ins.then_inc(w_done, 1)

            def score_spread_2(g):
                if not has(g):
                    return
                pe.wait_ge(diag2_ready, 2 * (g + 1))
                if has(g + 2):
                    pe.wait_ge(sm1, 9 * (g + 2) + 2)
                ps = light[0][:, 0, 0:T * N]
                mm(ps, ident_b, mask_b[:, 0].rearrange("p h m -> p (h m)"), start=True, stop=False)
                for i in range(2):
                    ins = mm(ps, block_ones, diag2[:, i].rearrange("p t m -> p (t m)"), start=False, stop=i == 1)
                ins.then_inc(s2_done, 1)

            def att2_transpose(g):
                if not has(g):
                    return
                pe.wait_ge(sm2, 9 * g + 9)
                if has(g + 2):
                    pe.wait_ge(pt_out, 2 * g + 5)
                elif not is_last(g):
                    pe.wait_ge(ff_sum, g)
                for t in range(T):
                    ins = nc.tensor.transpose(back(g)[:, 0, t * P:(t + 1) * P], att2[:, t], ident)
                ins.then_inc(pt2_done, 1)

            def attend_2(g):
                if not has(g):
                    return
                pe.wait_ge(pt2_lo, g + 1)
                pe.wait_ge(w_lo_s, 2 * g + 2)
                for t in range(T):
                    ins = three(tiles(back(g), O)[:, t], [((att2T_hi[:, t], att2T_lo[:, t]), (wh_hi[:, t], wh_lo[:, t]))])
                ins.then_inc(o_done, 1)

            def out_transpose(g):
                if not has(g):
                    return
                pe.wait_ge(o_elu, g + 1)
                for _, o in parts(g):
                    for ot in range(o.start, o.stop):
                        for t in range(T):
                            ins = nc.tensor.transpose(back(g)[:, ot, t * P:(t + 1) * P], o_place(g)[:, t, ot * P:(ot + 1) * P],
                                                      ident)
                    ins.then_inc(ot_done, 1)

            def ffn_in(g):
                if not has(g):
                    return
                pe.wait_ge(ol_done, g + 1)
                hi, lo = o_parts(g)
                for _, r in parts(g):
                    for ft in range(r.start, r.stop):
                        f = slice(ft * P, (ft + 1) * P)
                        for ot in range(OT):
                            if is_last(g) and ft == 0 and ot == 1:
                                pe.wait_ge(ol_done, g + 2)
                            ins = three(back(g)[:, ft], [((w1_hi[:, ot, f], w1_lo[:, ot, f]), (hi[:, ot], lo[:, ot]))],
                                        first=ot == 0, last=ot == OT - 1)
                    ins.then_inc(h1_done, 1)

            def ffn_out(g):
                if not has(g):
                    return
                pe.wait_ge(h1l_done, g + len(parts(g)))
                ps = tiles(back(g), O)
                hi, lo = h1_parts(g)
                for _, u in parts(g):
                    for t in range(2 * u.start, 2 * u.stop):
                        n = slice(t * P, (t + 1) * P)
                        mm(ps[:, t], ones_b, b2_rows, start=True, stop=False)
                        ins = three(ps[:, t], [((hi[:, ft, n], lo[:, ft, n]), (w2_hi[:, ft], w2_lo[:, ft]))
                                               for ft in range(OT)], first=False)
                    ins.then_inc(ff_done, 1)

            def period(p):
                if isinstance(p, int) and p == 0:
                    pe.wait_ge(s_weights, 5)
                if isinstance(p, int) and p == 1:
                    pe.wait_ge(s_b2, 1)
                head(p, 0)
                if isinstance(p, int) and p == 1:
                    head(p, 1)
                    score_spread_2(p - 1)
                else:
                    score_spread_2(p - 1)
                    head(p, 1)
                if isinstance(p, int) and p == 0:
                    head(p, 2)
                    head(p, 3)
                    att_transpose(p + 1, 1)
                    att_transpose(p + 1, 0)
                else:
                    att_transpose(p + 1, 1)
                    head(p, 2)
                    att_transpose(p + 1, 0)
                    head(p, 3)
                x_transpose(p + 2)
                attend(p + 1, 0)
                att2_transpose(p - 1)
                score_terms(p + 2)
                attend(p + 1, 1)
                attend_2(p - 1)
                attend(p + 1, 2)
                attend(p + 1, 3)
                score_spread(p + 2)
                project(p, 0)
                ffn_in(p - 1)
                project(p, 1)
                ffn_out(p - 1)

            x_transpose(0)
            score_terms(0)
            score_spread(0)
            x_transpose(1)
            score_terms(1)
            att_transpose(0, 1)
            att_transpose(0, 0)
            attend(0, 0)
            attend(0, 1)
            attend(0, 2)
            attend(0, 3)
            score_spread(1)
            periods(pe, period)

            g = LAST
            head(g, 0)
            score_spread_2(g - 1)
            head(g, 1)
            head(g, 2)
            head(g, 3)
            att2_transpose(g - 1)
            attend_2(g - 1)
            project(g, 0)
            project(g, 1)
            ffn_in(g - 1)
            score_spread_2(g)
            att2_transpose(g)
            attend_2(g)
            ffn_out(g - 1)
            out_transpose(g)
            ffn_in(g)
            ffn_out(g)


INPUTS = ["x", "adj", "L0_gnn_W_heads", "L0_gnn_a_heads", "L0_gnn_W_out", "L0_gnn_a_out", "L0_gnn_w1", "L0_gnn_b1",
          "L0_gnn_w2", "L0_gnn_b2", "L0_gnn_ln_gamma", "L0_gnn_ln_beta"]


def kernel(**inputs):
    import numpy as _np
    import concourse.bacc as _bacc
    from concourse import mybir as _mybir
    from concourse.bass_utils import run_bass_kernel_spmd as _run

    nc = _bacc.Bacc("TRN2", target_bir_lowering=False, num_devices=1)
    arrays, args = {}, []
    for name in INPUTS:
        a = _np.ascontiguousarray(inputs[name])
        arrays[f"in_{name}"] = a
        args.append(nc.dram_tensor(f"in_{name}", a.shape, _mybir.dt.from_np(a.dtype), kind="ExternalInput").ap())
    shape = inputs["x"].shape
    args.append(nc.dram_tensor("out_0", shape, _mybir.dt.float32, kind="ExternalOutput").ap())
    build(nc, *args)
    return _run(nc, [arrays], core_ids=[0]).results[0]["out_0"]
```
